# Optimizing a Trainium2 kernel written in Bass

```python
import numpy as np
import jax
import jax.numpy as jnp

def _softmax(x, axis=-1):
    return jax.nn.softmax(x, axis=axis)

def _gelu(x):
    return jax.nn.gelu(x, approximate=True)

def _silu(x):
    return jax.nn.silu(x)

def _sigmoid(x):
    return jax.nn.sigmoid(x)

def _layernorm(x, axis=-1, eps=1e-05):
    m = jnp.mean(x, axis=axis, keepdims=True)
    v = jnp.var(x, axis=axis, keepdims=True)
    return (x - m) / jnp.sqrt(v + eps)

def _scatter_add(tgt, idx, src, axis=0):
    return tgt.at[idx].add(src)

def _segment_sum(src, seg, n):
    return jax.ops.segment_sum(src, seg, n)
kernel_name = 'mk_adj_resnorm_d2_adj_r2_7bc189'

def setup_inputs(seed: int=0):
    np.random.seed(seed)
    _w = jnp.asarray

    def _rec_inputs():
        import jax
        import jax.numpy as jnp
        _gk = jax.random.key(seed)
        x = -0.000125 + 0.9999 * jax.random.normal(jax.random.fold_in(_gk, 1), (128, 64, 512), jnp.float32)
        _w = (1.0 + jnp.arange(64, dtype=jnp.float32)) ** (-0.5)
        _w = _w / _w.mean()
        _pij = jnp.clip(0.125 * _w[:, None] * _w[None, :], 0.0, 1.0)
        _a = jax.random.uniform(jax.random.fold_in(_gk, 2), (128, 64, 64)) < _pij
        _a = jnp.logical_or(_a, jnp.swapaxes(_a, -1, -2))
        _a = jnp.logical_or(_a, jnp.eye(64, dtype=bool))
        _af = _a.astype(jnp.float32)
        _af = _af * jax.random.uniform(jax.random.fold_in(_gk, 3), (128, 64, 64), jnp.float32, 0.05, 0.999994)
        adj = _af
        return (x, adj)
    x, adj = _rec_inputs()

    def _L0_gnn_setup():
        import jax, jax.numpy as jnp
        import numpy as np
        B, N, H, E = (64, 256, 512, 4)
        BN_EPS = 1e-05
        key = jax.random.key(seed)
        ks = jax.random.split(key, 6)
        x = jax.random.normal(ks[0], (B, N, H), dtype=jnp.float32)
        adj = jax.random.uniform(ks[1], (B, N, N), dtype=jnp.float32)
        stdv = 1.0 / np.sqrt(H)
        expert_w = jax.random.uniform(ks[2], (E, H, H), minval=-stdv, maxval=stdv, dtype=jnp.float32)
        r_std = 1.0 / np.sqrt(H)
        router_w = jax.random.uniform(ks[3], (H, E), minval=-r_std, maxval=r_std, dtype=jnp.float32)
        router_b = jax.random.uniform(ks[4], (E,), minval=-r_std, maxval=r_std, dtype=jnp.float32)
        bn_gamma = jnp.ones((E, H), dtype=jnp.float32)
        bn_beta = jnp.zeros((E, H), dtype=jnp.float32)
        return {'x': x, 'adj': adj, 'router_w': router_w, 'router_b': router_b, 'expert_w': expert_w, 'bn_gamma': bn_gamma, 'bn_beta': bn_beta}
    _L0_gnn_all = _L0_gnn_setup()
    _L0_gnn_in = {k: v for k, v in _L0_gnn_all.items() if k in ('router_w', 'router_b', 'expert_w', 'bn_gamma', 'bn_beta')}
    del _L0_gnn_all

    def _L1_gnn_setup():
        import jax, jax.numpy as jnp
        import numpy as np
        NUM_HEADS = 16
        key = jax.random.key(seed)
        ks = jax.random.split(key, 7)
        B, N, D = (16, 256, 512)
        return {'x': jax.random.normal(ks[0], (B, N, D), dtype=jnp.float32), 'spatial_encoding': jax.random.normal(ks[1], (B, N, N), dtype=jnp.float32), 'edge_encoding': jax.random.normal(ks[2], (B, N, N), dtype=jnp.float32), 'Wq': jax.random.normal(ks[3], (D, D), dtype=jnp.float32) * D ** (-0.5), 'Wk': jax.random.normal(ks[4], (D, D), dtype=jnp.float32) * D ** (-0.5), 'Wv': jax.random.normal(ks[5], (D, D), dtype=jnp.float32) * D ** (-0.5), 'Wo': jax.random.normal(ks[6], (D, D), dtype=jnp.float32) * D ** (-0.5)}
    _L1_gnn_all = _L1_gnn_setup()
    _L1_gnn_in = {k: v for k, v in _L1_gnn_all.items() if k in ('Wq', 'Wk', 'Wv', 'Wo')}
    del _L1_gnn_all
    return {'x': x, 'adj': adj, 'L0_gnn_router_w': _L0_gnn_in['router_w'], 'L0_gnn_router_b': _L0_gnn_in['router_b'], 'L0_gnn_expert_w': _L0_gnn_in['expert_w'], 'L0_gnn_bn_gamma': _L0_gnn_in['bn_gamma'], 'L0_gnn_bn_beta': _L0_gnn_in['bn_beta'], 'L1_gnn_Wq': _L1_gnn_in['Wq'], 'L1_gnn_Wk': _L1_gnn_in['Wk'], 'L1_gnn_Wv': _L1_gnn_in['Wv'], 'L1_gnn_Wo': _L1_gnn_in['Wo']}

def reference(x, adj, L0_gnn_router_w, L0_gnn_router_b, L0_gnn_expert_w, L0_gnn_bn_gamma, L0_gnn_bn_beta, L1_gnn_Wq, L1_gnn_Wk, L1_gnn_Wv, L1_gnn_Wo):
    import jax
    import jax.numpy as jnp

    def _L0_gnn_ref(x, adj, router_w, router_b, expert_w, bn_gamma, bn_beta):
        import jax, jax.numpy as jnp
        import numpy as np
        B, N, H, E = (64, 256, 512, 4)
        BN_EPS = 1e-05
        scores = x.mean(axis=1) @ router_w + router_b
        top1 = jnp.argmax(scores, axis=-1)
        n_exp = expert_w.shape[0]
        W = expert_w[top1]
        support = jnp.einsum('bnh,bhk->bnk', x, W)
        out = jnp.einsum('bnm,bmk->bnk', adj, support)
        s = jax.ops.segment_sum(out.sum(axis=1), top1, num_segments=n_exp)
        ss = jax.ops.segment_sum((out * out).sum(axis=1), top1, num_segments=n_exp)
        cnt = jax.ops.segment_sum(jnp.ones_like(top1, dtype=out.dtype), top1, num_segments=n_exp) * out.shape[1]
        cnt = jnp.maximum(cnt, 1.0)[:, None]
        mean = s / cnt
        var = ss / cnt - mean * mean
        m = mean[top1][:, None, :]
        inv = jax.lax.rsqrt(var[top1][:, None, :] + BN_EPS)
        y = (out - m) * inv * bn_gamma[top1][:, None, :] + bn_beta[top1][:, None, :]
        return jax.nn.relu(y)

    def _L1_gnn_ref(x, spatial_encoding, edge_encoding, Wq, Wk, Wv, Wo):
        import jax, jax.numpy as jnp
        import numpy as np
        NUM_HEADS = 16
        B, N, D = x.shape
        H = NUM_HEADS
        hd = D // H
        scale = D ** (-0.5)

        def split_heads(t):
            return t.reshape(B, N, H, hd).transpose(0, 2, 1, 3)
        q = split_heads(x @ Wq.T)
        k = split_heads(x @ Wk.T)
        v = split_heads(x @ Wv.T)
        bias = (spatial_encoding + edge_encoding)[:, None]
        a = jnp.einsum('bhnd,bhmd->bhnm', q, k) * scale + bias
        row_nonzero = jnp.any(a != 0, axis=-1, keepdims=True)
        a = jnp.where(row_nonzero, a, -jnp.inf)
        p = jax.nn.softmax(a, axis=-1)
        p = jnp.where(jnp.isnan(p), 0.0, p)
        o = jnp.einsum('bhnm,bhmd->bhnd', p, v)
        o = o.transpose(0, 2, 1, 3).reshape(B, N, D)
        return o @ Wo.T
    x = _layernorm(x + _L0_gnn_ref(x, adj, L0_gnn_router_w, L0_gnn_router_b, L0_gnn_expert_w, L0_gnn_bn_gamma, L0_gnn_bn_beta), axis=-1)
    x = _layernorm(x + _L1_gnn_ref(x, adj, adj, L1_gnn_Wq, L1_gnn_Wk, L1_gnn_Wv, L1_gnn_Wo), axis=-1)
    return x

_drawn_inputs = setup_inputs


def setup_inputs(seed=0):
    import zlib

    import numpy as np

    out = dict(_drawn_inputs(seed))
    spreads = {'L0_gnn_bn_gamma': (1.0, 0.2), 'L0_gnn_bn_beta': (0.0, 0.1)}
    factors = {}
    for name, (base, spread) in spreads.items():
        noise = np.random.default_rng([zlib.crc32(name.encode()), seed]).standard_normal(out[name].shape)
        drawn = base * np.exp(spread * noise) if base else spread * noise
        out[name] = jnp.asarray(drawn.astype(out[name].dtype))
    for name, factor in factors.items():
        out[name] = (out[name] * factor).astype(out[name].dtype)
    return out
```

```python
from contextlib import ExitStack

import numpy as np

import concourse.bass as bass
from concourse import mybir
from concourse.bass import ds

F32 = mybir.dt.float32
F32R = mybir.dt.float32r
I32 = mybir.dt.int32
ALU = mybir.AluOpType
ACT = mybir.ActivationFunctionType
AX = mybir.AxisListType

P = 128
EPS = 1e-5


class Quad:

    def __init__(self, k, i=None, unroll=1):
        self.k, self.i, self.unroll = k, i, unroll

    def __add__(self, n):
        return Quad(self.k + n, self.i, self.unroll)

    def value(self, per_quad, extra=0):
        if self.i is None:
            return per_quad * self.k + extra
        return self.i * (per_quad * self.unroll) + (per_quad * self.k + extra)

    def turn(self, n, per_turn, extra=0):
        if self.i is None:
            return per_turn * (self.k // n) + extra
        return self.i * (per_turn * (self.unroll // n)) + (per_turn * (self.k // n) + extra)

    def slot(self, n):
        return self.k % n

    def before(self, n):
        return self.i is None and self.k < n


def steps(eng, body, first, loop_from, loop_to, last, unroll):
    for s in range(first, loop_from):
        body(Quad(s))
    assert (loop_to - loop_from) % unroll == 0
    with eng.Fori(0, (loop_to - loop_from) // unroll) as i:
        for u in range(unroll):
            body(Quad(loop_from + u, i, unroll))
    for s in range(loop_to, last + 1):
        body(Quad(s))


def graph_layers(nc, x, adj, adjT, router_w, router_b, expert_w, gamma, beta, wqT, wkT, wvT, woT, out):
    B, N, D = x.shape
    E = expert_w.shape[0]
    H = 16
    HD = D // H
    C = D // P
    HC = P // HD
    TN = 2 * N
    NQ = B // 4
    SCALE = float(D) ** -0.5
    NT = 3
    assert TN == P and D == 512 and E == 4

    x_q = x.rearrange("(q t g) n d -> q (g n) t d", t=2, g=2)
    out_q = out.rearrange("(q t g) n d -> q t (g n) d", t=2, g=2)
    adj_q = adj.rearrange("(q t g) n m -> q (g n) t m", t=2, g=2)
    adjT_q = adjT.rearrange("(q t g) m n -> q g m t n", t=2, g=2)

    z_dram = nc.dram_tensor("z_scratch", [NQ, P, 2, D], F32, kind="Internal").ap()

    outer = ExitStack()
    with outer:
        def sem(name):
            return outer.enter_context(nc.semaphore(name))

        ps = outer.enter_context(nc.psum_tensor("ps", [P, 8, 512], F32))

        def sb(stack, name, shape, dt=F32):
            return stack.enter_context(nc.sbuf_tensor(name, shape, dt))

        wp_h = sb(outer, "wp_h", [P, 4, C, D], F32R)
        wp_l = sb(outer, "wp_l", [P, 4, C, D], F32R)
        tab = sb(outer, "tab", [P, 2, E, D])
        ident = sb(outer, "ident", [P, P])
        expert = sb(outer, "expert", [4, NQ], I32)
        minus_half = sb(outer, "minus_half", [P, D])

        with ExitStack() as st:
            we_h = sb(st, "we_h", [P, E, C, D], F32R)
            we_l = sb(st, "we_l", [P, E, C, D], F32R)
            raw = sb(st, "raw", [P, 2, 2, D])
            xa = sb(st, "xa", [P, 2, 2, D])
            aT = sb(st, "aT", [P, 2, 2, P + 2])
            yh = [sb(st, f"yh{p}", [P, 2, C, 3 * N], F32R) for p in range(2)]
            yl = [sb(st, f"yl{p}", [P, 2, C, 3 * N], F32R) for p in range(2)]
            z = sb(st, "z", [P, 2, 2, D])
            z2 = sb(st, "z2", [P, 2, D])
            xsum = sb(st, "xsum", [P, 2, C, 4])
            rw = sb(st, "rw", [P, C, E])
            rb = sb(st, "rb", [4, E])
            eid = sb(st, "eid", [4, E])
            score = sb(st, "score", [4, E])
            best = sb(st, "best", [4, 1])
            hit = sb(st, "hit", [4, E])
            first_hit = sb(st, "first_hit", [4, 1])
            expert_f = sb(st, "expert_f", [4, NQ])
            is_e = sb(st, "is_e", [4, E, NQ])
            count_g = sb(st, "count_g", [4, E])
            ones4 = sb(st, "ones4", [4, 1])
            pick = sb(st, "pick", [P, E, 4])
            count = sb(st, "count", [4, 2])
            gam, bet = raw[0:4, 0, 0, :], raw[0:4, 0, 1, :]
            bn = z[0:4, :, :, :].rearrange("p a t d -> p (a t) d")

            psY = [ps[:, 2 * t:2 * t + 2, :].rearrange("p b (c n) -> p (b c) n", c=2) for t in range(2)]
            psZ = [ps[:, 4 + t, :] for t in range(2)]
            psR = ps[0:4, 6, 0:E]
            psCnt = ps[0:4, 6, 16:17]
            psSum = [ps[0:4, 4 + k, :] for k in range(2)]

            w_loaded = [sem(f"w_loaded{p}") for p in range(2)]
            w_high = sem("w_high")
            w_low = sem("w_low")
            small_loaded = sem("small_loaded")
            xa_loaded = [sem(f"xa_loaded{p}") for p in range(2)]
            aT_ready = sem("aT_ready")
            consts1 = sem("consts1")
            pool_consts = sem("pool_consts")
            tab_zero = sem("tab_zero")
            y_done = sem("y_done")
            yh_done = sem("yh_done")
            xsum_done = sem("xsum_done")
            yl_done = sem("yl_done")
            r_done = sem("r_done")
            route = sem("route")
            ROUTE = 6
            z_done = sem("z_done")
            z_copied = sem("z_copied")
            z_squared = sem("z_squared")
            summed = sem("summed")
            z_stored = [sem(f"z_stored{p}") for p in range(2)]
            sums_out = sem("sums_out")
            cnt_in = sem("cnt_in")
            bn_loaded = sem("bn_loaded")
            bn_step = sem("bn_step")
            bn_root = sem("bn_root")
            spread = sem("spread")
            tab_set = sem("tab_set")

            half = C // 2
            sources = [expert_w[e] for e in range(E)] + [wqT, wkT, wvT, woT]

            def weight_half(n):
                m, hf = n // 2, n % 2
                src = sources[m].rearrange("(c p) d -> p c d", p=P)[:, hf * half:(hf + 1) * half, :]
                hi, lo, j = (we_h, we_l, m) if m < E else (wp_h, wp_l, m - E)
                c = slice(hf * half, (hf + 1) * half)
                return src, hi[:, j, c, :], lo[:, j, c, :]

            NW = 2 * len(sources)

            def both_loaded(eng, q):
                eng.wait_ge(xa_loaded[q.slot(2)], q.turn(2, 48, 48))

            with nc.Block() as block:

                @block.sync
                def _(sp):
                    def load(q):
                        p = q.slot(2)
                        sp.dma_start(xa[:, p, :, :], x_q[ds(q.value(1), 1)].rearrange("a p t d -> (a p) t d")
                                     ).then_inc(xa_loaded[p], 16)
                        for g in range(2):
                            sp.dma_start(aT[g * N:(g + 1) * N, p, :, g * N:(g + 1) * N],
                                         adjT_q[ds(q.value(1), 1), g].rearrange("a m t n -> (a m) t n")
                                         ).then_inc(xa_loaded[p], 16)

                    sp.wait_ge(aT_ready, 1)
                    load(Quad(0))
                    load(Quad(1))
                    sp.dma_start(rw[:], router_w.rearrange("(c p) e -> p c e", p=P)).then_inc(small_loaded, 16)
                    sp.dma_start(rb[:], router_b.rearrange("(a e) -> a e", a=1).to_broadcast([4, E])
                                 ).then_inc(small_loaded, 16)
                    for n in range(NW):
                        if n >= 2:
                            sp.wait_ge(w_low, n - 1)
                        sp.dma_start(raw[:, n % 2, :, :], weight_half(n)[0]).then_inc(w_loaded[n % 2], 16)

                    sp.wait_ge(w_low, NW)
                    sp.dma_start(gam, gamma).then_inc(bn_loaded, 16)
                    sp.dma_start(bet, beta).then_inc(bn_loaded, 16)

                    def step(q, more=True):
                        if more:
                            sp.wait_ge(y_done, q.value(2, 2))
                            load(q + 2)
                        sp.wait_ge(z_copied, q.value(2, 2))
                        sp.dma_start(z_dram[ds(q.value(1), 1)].rearrange("a p t d -> (a p) t d"),
                                     z[:, q.slot(2), :, :]).then_inc(z_stored[q.slot(2)], 16)

                    steps(sp, step, 0, 0, NQ - 2, NQ - 3, 2)
                    for s in range(NQ - 2, NQ):
                        step(Quad(s), more=False)
                    for p in range(2):
                        sp.wait_ge(z_stored[p], 16 * (NQ // 2))

                @block.gpsimd
                def _(pool):
                    nc.gpsimd.memset(ident[:], 0.0).then_inc(pool_consts, 1)
                    nc.gpsimd.memset(tab[:], 0.0).then_inc(tab_zero, 1)
                    pool.wait_ge(pool_consts, 1)
                    nc.gpsimd.affine_select(out=ident[:], in_=ident[:], compare_op=ALU.not_equal, fill=1.0,
                                            base=0, pattern=[[-1, P]], channel_multiplier=1).then_inc(pool_consts, 1)
                    nc.gpsimd.memset(minus_half[:], -0.5).then_inc(pool_consts, 1)
                    pool.wait_ge(tab_zero, 1)
                    pool.wait_ge(pool_consts, 3)

                    def step(q):
                        pool.wait_ge(route, q.value(ROUTE, ROUTE))
                        for t in range(2):
                            e = [pool.value_load(expert[2 * t + g:2 * t + g + 1, ds(q.value(1), 1)],
                                                 min_val=0, max_val=E - 1) for g in range(2)]
                            if not (q.before(1) and t == 0):
                                pool.wait_ge(summed, q.value(8, 4 * t))
                            pool.wait_ge(z_copied, q.value(2, t + 1))
                            for k, src in enumerate((z[:, q.slot(2), t, :], z2[:, t, :])):
                                if k == 1:
                                    pool.wait_ge(z_squared, q.value(2, t + 1))
                                for g in range(2):
                                    rows = slice(g * N, (g + 1) * N)
                                    if k or g:
                                        pool.wait_ge(summed, q.value(8, 4 * t + 2 * k + g))
                                    acc = tab[rows, k, ds(e[g], 1), :].rearrange("p a d -> p (a d)")
                                    nc.gpsimd.tensor_tensor(acc, acc, src[rows, :], ALU.add).then_inc(summed, 1)

                    steps(pool, step, 0, 2, NQ, NQ - 1, 2)
                    pool.wait_ge(bn_step, 7)
                    nc.gpsimd.tensor_tensor(bn[:, 1, :], bn[:, 1, :], minus_half[0:4, :], ALU.pow).then_inc(bn_root, 1)

                @block.scalar
                def _(act):
                    def y_high(q):
                        p = q.slot(2)
                        for t in range(2):
                            act.wait_ge(y_done, q.value(2, t + 1))
                            if not q.before(2):
                                act.wait_ge(z_done, q.value(2, t - 3))
                            nc.scalar.activation(
                                yh[p][:, t, :, :].rearrange("p c (s n) -> p c s n", s=3)[:, :, 0:3:2, :],
                                psY[t][:, :, 0:P].rearrange("p c (g n) -> p c g n", g=2), ACT.Copy).then_inc(yh_done, 1)

                    def act_step(s):
                        if s.i is not None or s.k < NQ - 1:
                            y_high(s + 1)
                        for t in range(2):
                            act.wait_ge(z_copied, s.value(2, t + 1))
                            if not s.before(1):
                                act.wait_ge(summed, s.value(8, 4 * t - 4))
                            nc.scalar.activation(z2[:, t, :], z[:, s.slot(2), t, :], ACT.Square).then_inc(z_squared, 1)

                    for n in range(NW):
                        _, hi, _ = weight_half(n)
                        act.wait_ge(w_loaded[n % 2], 16 * (n // 2 + 1))
                        nc.scalar.activation(hi, raw[:, n % 2, :, :], ACT.Copy).then_inc(w_high, 1)
                        if n == 1:
                            act.wait_ge(consts1, 2)
                            y_high(Quad(0))

                    steps(act, act_step, 0, 2, NQ - 2, NQ - 1, 2)
                    for k in range(2):
                        for e in range(E):
                            act.wait_ge(spread, k * E + e + 1)
                            nc.scalar.activation(tab[:, k, e, :], ps[:, (k * E + e) % 4, :], ACT.Copy).then_inc(tab_set, 1)

                @block.vector
                def _(dve):
                    nc.vector.memset(aT[:], 0.0).then_inc(consts1, 1)
                    dve.wait_ge(consts1, 1)
                    for g in range(2):
                        ins = nc.vector.memset(aT[g * N:(g + 1) * N, :, :, P + g:P + g + 1], 1.0)
                    ins.then_inc(aT_ready, 1)
                    for t_ in (*yh, *yl):
                        nc.vector.memset(t_[:].bitcast(F32), 0.0)
                    nc.vector.memset(ones4[:], 1.0)
                    nc.vector.memset(pick[:], 0.0).then_inc(bn_step, 1)
                    dve.wait_ge(bn_step, 1)
                    for e in range(E):
                        nc.vector.memset(pick[:, e, e:e + 1], 1.0)
                        ins = nc.vector.memset(eid[:, e:e + 1], float(e - E))
                    ins.then_inc(consts1, 1)

                    def y_low(q):
                        p = q.slot(2)
                        for t in range(2):
                            dve.wait_ge(yh_done, q.value(2, t + 1))
                            if not q.before(2):
                                dve.wait_ge(r_done, q.value(1, -1))
                            nc.vector.tensor_copy(xsum[:, p, :, 2 * t:2 * t + 2], psY[t][:, :, P:P + 2]).then_inc(xsum_done, 1)
                            yy = [a[p][:, t, :, :].rearrange("p c (s n) -> p c s n", s=3)[:, :, 0:3:2, :] for a in (yh, yl)]
                            nc.vector.tensor_tensor(yy[1], psY[t][:, :, 0:P].rearrange("p c (g n) -> p c g n", g=2),
                                                    yy[0], ALU.subtract).then_inc(yl_done, 1)

                    def choose(q):
                        n = 0

                        def link(ins):
                            nonlocal n
                            n += 1
                            ins.then_inc(route, 1)
                            if n < ROUTE:
                                dve.wait_ge(route, q.value(ROUTE, n))

                        dve.wait_ge(r_done, q.value(1, 1))
                        link(nc.vector.scalar_tensor_tensor(out=score[:], in0=psR, scalar=1.0 / N, in1=rb[:],
                                                            op0=ALU.mult, op1=ALU.add))
                        link(nc.vector.tensor_reduce(best[:], score[:], AX.X, ALU.max))
                        link(nc.vector.scalar_tensor_tensor(out=hit[:], in0=score[:], scalar=best[:, 0:1], in1=eid[:],
                                                            op0=ALU.is_ge, op1=ALU.mult))
                        link(nc.vector.tensor_reduce(first_hit[:], hit[:], AX.X, ALU.min))
                        link(nc.vector.tensor_scalar(expert_f[:, ds(q.value(1), 1)], first_hit[:], float(E), None, ALU.add))
                        link(nc.vector.tensor_scalar(expert[:, ds(q.value(1), 1)], first_hit[:], float(E), None, ALU.add))

                    def z_copy(q, t):
                        dve.wait_ge(z_done, q.value(2, t + 1))
                        if not q.before(2):
                            dve.wait_ge(z_stored[q.slot(2)], q.turn(2, 16))
                            dve.wait_ge(summed, q.value(8, 4 * t - 12))
                            dve.wait_ge(z_squared, q.value(2, t - 3))
                        nc.vector.tensor_copy(z[:, q.slot(2), t, :], psZ[t]).then_inc(z_copied, 1)

                    def split_low(n):
                        _, hi, lo = weight_half(n)
                        dve.wait_ge(w_high, n + 1)
                        nc.vector.tensor_tensor(lo, raw[:, n % 2, :, :], hi, ALU.subtract).then_inc(w_low, 1)

                    split_low(0)
                    split_low(1)
                    y_low(Quad(0))
                    dve.wait_ge(small_loaded, 32)
                    dve.wait_ge(consts1, 2)
                    choose(Quad(0))
                    for n in range(2, NW):
                        split_low(n)

                    def step(s):
                        more = s.i is not None or s.k < NQ - 1
                        if more:
                            y_low(s + 1)
                        z_copy(s, 0)
                        if more:
                            choose(s + 1)
                        z_copy(s, 1)

                    steps(dve, step, 0, 2, NQ - 2, NQ - 1, 2)

                    chain = [1]

                    def link(ins):
                        chain[0] += 1
                        ins.then_inc(bn_step, 1)
                        dve.wait_ge(bn_step, chain[0])

                    dve.wait_ge(route, ROUTE * NQ)
                    for e in range(E):
                        ins = nc.vector.tensor_scalar(is_e[:, e, :], expert_f[:], float(e), None, ALU.is_equal)
                    link(ins)
                    nc.vector.tensor_reduce(count_g[:], is_e[:], AX.X, ALU.add).then_inc(cnt_in, 1)
                    dve.wait_ge(sums_out, 1)
                    link(nc.vector.tensor_scalar(count[:, 0:1], psCnt, float(N), 1.0, ALU.mult, ALU.max))
                    link(nc.vector.reciprocal(count[:, 1:2], count[:, 0:1]))
                    dve.wait_ge(bn_loaded, 32)
                    for p in range(2):
                        dve.wait_ge(z_stored[p], 16 * (NQ // 2))
                    dve.wait_ge(sums_out, 3)
                    nc.vector.tensor_scalar(bn[:, 0, :], psSum[0], count[:, 1:2], None, ALU.mult)
                    link(nc.vector.tensor_scalar(bn[:, 1, :], psSum[1], count[:, 1:2], None, ALU.mult))
                    link(nc.vector.tensor_tensor(bn[:, 2, :], bn[:, 0, :], bn[:, 0, :], ALU.mult))
                    link(nc.vector.scalar_tensor_tensor(out=bn[:, 1, :], in0=bn[:, 1, :], scalar=EPS, in1=bn[:, 2, :],
                                                        op0=ALU.add, op1=ALU.subtract))
                    dve.wait_ge(bn_root, 1)
                    link(nc.vector.tensor_tensor(bn[:, 2, :], bn[:, 1, :], gam, ALU.mult))
                    link(nc.vector.tensor_tensor(bn[:, 0, :], bn[:, 0, :], bn[:, 2, :], ALU.mult))
                    link(nc.vector.tensor_tensor(bn[:, 3, :], bet, bn[:, 0, :], ALU.subtract))

                @block.tensor
                def _(pe):
                    def y_products(q):
                        both_loaded(pe, q)
                        p = q.slot(2)
                        for t in range(2):
                            if not q.before(1):
                                pe.wait_ge(yl_done, q.value(2, t - 1))
                            for c in range(C):
                                ins = pe.matmul(psY[t][:, c, 0:P + 2], xa[:, p, t, c * P:(c + 1) * P], aT[:, p, t, :],
                                                start=True, stop=True, skip_group_check=True)
                            ins.then_inc(y_done, 1)

                    def routing(q):
                        pe.wait_ge(xsum_done, q.value(2, 2))
                        if not q.before(1):
                            pe.wait_ge(route, q.value(ROUTE, 1 - ROUTE))
                        for c in range(C):
                            ins = pe.matmul(psR, xsum[:, q.slot(2), c, :], rw[:, c, :], start=(c == 0), stop=(c == C - 1))
                        ins.then_inc(r_done, 1)

                    def z_products(q, t):
                        p = q.slot(2)
                        e = [pe.value_load(expert[2 * t + g:2 * t + g + 1, ds(q.value(1), 1)],
                                           min_val=0, max_val=E - 1) for g in range(2)]
                        if not q.before(1):
                            pe.wait_ge(z_copied, q.value(2, t - 1))
                        n = 0
                        for g in range(2):
                            for ya, wa in ((yh, we_h), (yh, we_l), (yl, we_h)):
                                for c in range(C):
                                    ins = pe.matmul(psZ[t], ya[p][:, t, c, g * N:g * N + P],
                                                    wa[:, ds(e[g], 1), c, :].rearrange("p a d -> p (a d)"),
                                                    start=(n == 0), stop=(n == 2 * NT * C - 1))
                                    n += 1
                        ins.then_inc(z_done, 1)

                    pe.wait_ge(aT_ready, 1)
                    y_products(Quad(0))
                    pe.wait_ge(small_loaded, 32)
                    routing(Quad(0))

                    def step(s):
                        more = s.i is not None or s.k < NQ - 1
                        if more:
                            y_products(s + 1)
                        pe.wait_ge(route, s.value(ROUTE, ROUTE))
                        pe.wait_ge(yl_done, s.value(2, 2))
                        z_products(s, 0)
                        if more:
                            routing(s + 1)
                        z_products(s, 1)

                    pe.wait_ge(w_low, NW)
                    steps(pe, step, 0, 2, NQ - 2, NQ - 1, 2)

                    pe.wait_ge(cnt_in, 1)
                    pe.matmul(psCnt, count_g[:], ones4[:], start=True, stop=True).then_inc(sums_out, 1)
                    pe.wait_ge(summed, 8 * NQ)
                    for k in range(2):
                        for e in range(E):
                            ins = pe.matmul(psSum[k], pick[:, e, :], tab[:, k, e, :], start=(e == 0), stop=(e == E - 1))
                        ins.then_inc(sums_out, 1)
                    pe.wait_ge(pool_consts, 3)
                    for k in range(2):
                        pe.wait_ge(bn_step, 8 if k == 0 else 10)
                        for e in range(E):
                            n = k * E + e
                            if n >= 4:
                                pe.wait_ge(tab_set, n - 3)
                            pe.matmul(ps[:, n % 4, :], ident[0:4, e:e + 1].to_broadcast([4, P]), bn[:, 2 + k, :],
                                      start=True, stop=True).then_inc(spread, 1)
        with ExitStack() as st:
            zx = sb(st, "zx", [P, 2, 2, D])
            x1 = sb(st, "x1", [P, 4, 2, D])
            xTh = sb(st, "xTh", [P, C, 2 * P], F32R)
            xTl = sb(st, "xTl", [P, C, 2 * P], F32R)
            qz = [sb(st, f"qz{p}", [P, C, 2, 3 * N]) for p in range(2)]
            kz = [sb(st, f"kz{p}", [P, C, 4, HC * N]) for p in range(2)]
            vz = [sb(st, f"vz{p}", [P, 2, H // 2, 2, 2 * HD]) for p in range(2)]
            adj_in = sb(st, "adj_in", [P, 2, N])
            adj2 = sb(st, "adj2", [P, 2, N])
            sc = sb(st, "sc", [P, 2, H, N])
            mx = sb(st, "mx", [P, 2, H])
            amx = sb(st, "amx", [P, 2, H])
            tot = sb(st, "tot", [P, 2, H])
            inv = sb(st, "inv", [P, 2, H])
            pT = sb(st, "pT", [P, H // 2, P])
            o = sb(st, "o", [P, 2, D])
            oTh = sb(st, "oTh", [P, 2, C, P], F32R)
            oTl = sb(st, "oTl", [P, 2, C, P], F32R)
            res = sb(st, "res", [P, 2, D])
            waiter = sb(st, "waiter", [P, 2])
            st1 = sb(st, "st1", [P, 2, 6])
            ag1 = sb(st, "ag1", [P, 2, 2])
            ve1 = sb(st, "ve1", [P, 2])
            rs1 = sb(st, "rs1", [P, 2])
            st2 = sb(st, "st2", [P, 2, 6])
            ag2 = sb(st, "ag2", [P, 2, 2])
            ve2 = sb(st, "ve2", [P, 2])
            rs2 = sb(st, "rs2", [P, 2])

            RING_XT, RING_Q, RING_K, RING_V, RING_OT, RING_O = (0, 1), (2, 3, 4, 5), (6, 7, 8, 9), (10, 11), (12, 14), (13, 15)

            def ring(use):
                return ps[:, use % 4, :]

            psS = ps[:, 4:6, :].rearrange("p b n -> p (b n)")
            psT = ps[:, 6:8, :].rearrange("p b (k n) -> p (b k) n", n=P)
            psO = ps[:, 4:6, :].rearrange("p b (k g n) -> p (b k) g n", g=2, n=2 * HD)

            zeros2 = sem("zeros2")
            zx_loaded = sem("zx_loaded")
            adj_loaded = sem("adj_loaded")
            out_stored = [sem(f"out_stored{t}") for t in range(2)]
            xT_done = sem("xT_done")
            q_done = sem("q_done")
            k_done = sem("k_done")
            v_done = sem("v_done")
            s_done = sem("s_done")
            pT_done = sem("pT_done")
            pv_done = sem("pv_done")
            oT_done = sem("oT_done")
            o_done = sem("o_done")
            xTh_done = sem("xTh_done")
            q_set = sem("q_set")
            k_set = sem("k_set")
            v_set = sem("v_set")
            exp_done = sem("exp_done")
            pT_set = sem("pT_set")
            oTh_done = sem("oTh_done")
            bn_applied = sem("bn_applied")
            root1 = sem("root1")
            root2 = sem("root2")
            shifted = sem("shifted")
            relu_res = sem("relu_res")
            stats1 = sem("stats1")
            aggr1 = sem("aggr1")
            var1 = sem("var1")
            x1_done = sem("x1_done")
            xTl_done = sem("xTl_done")
            adj2_done = sem("adj2_done")
            biased = sem("biased")
            max_done = sem("max_done")
            absmax_done = sem("absmax_done")
            tot_done = sem("tot_done")
            tot_inv = sem("tot_inv")
            inv_done = sem("inv_done")
            o_normed = sem("o_normed")
            oTl_done = sem("oTl_done")
            res_done = sem("res_done")
            stats2 = sem("stats2")
            aggr2 = sem("aggr2")
            var2 = sem("var2")
            out_done = sem("out_done")

            def pipeline(eng, body):
                def step(s):
                    known = s.i is None
                    a = s + 1 if not known or 0 <= s.k + 1 < NQ else None
                    b = s if not known or 0 <= s.k < NQ else None
                    c = s + -1 if not known or 0 <= s.k - 1 < NQ else None
                    body(a, b, c)
                steps(eng, step, -1, 3, NQ - 1, NQ, 4)

            with nc.Block() as block:

                @block.sync
                def _(sp):
                    def load(q):
                        row = ds(q.value(1), 1)
                        sp.dma_start(zx[:, 0, :, :], z_dram[row].rearrange("a p t d -> (a p) t d")).then_inc(zx_loaded, 16)
                        sp.dma_start(zx[:, 1, :, :], x_q[row].rearrange("a p t d -> (a p) t d")).then_inc(zx_loaded, 16)

                    def body(a, b, c):
                        if b is not None:
                            if not b.before(1):
                                sp.wait_ge(adj2_done, b.value(1))
                            sp.dma_start(adj_in[:], adj_q[ds(b.value(1), 1)].rearrange("a p t m -> (a p) t m")
                                         ).then_inc(adj_loaded, 16)
                        if a is not None:
                            if not a.before(1):
                                sp.wait_ge(relu_res, a.value(2))
                            load(a)
                        if c is not None:
                            for t in range(2):
                                sp.wait_ge(out_done, c.value(2, t + 1))
                                sp.dma_start(out_q[ds(c.value(1), 1), t].rearrange("a p d -> (a p) d"),
                                             res[:, t, :]).then_inc(out_stored[t], 16)

                    pipeline(sp, body)
                    for t in range(2):
                        sp.wait_ge(out_stored[t], 16 * NQ)

                @block.gpsimd
                def _(pool):
                    def shift(q, t):
                        if t == 1 and (q.i is not None or q.k + 2 < NQ):
                            pool.wait_ge(bn_applied, (q + 2).value(8, 4))
                        pool.wait_ge(max_done, q.value(2, t + 1))
                        pool.wait_ge(absmax_done, q.value(2, t + 1))
                        nc.gpsimd.tensor_tensor(sc[:, t, :, :], sc[:, t, :, :],
                                                mx[:, t, :].unsqueeze(2).to_broadcast([P, H, N]),
                                                ALU.subtract).then_inc(shifted, 1)

                    def batch_norm(q, t):
                        e = [pool.value_load(expert[2 * t + g:2 * t + g + 1, ds(q.value(1), 1)],
                                             min_val=0, max_val=E - 1) for g in range(2)]
                        pool.wait_ge(zx_loaded, q.value(32, 32))
                        if q.i is not None or q.k >= 2:
                            pool.wait_ge(shifted, (q + -2).value(2, t + 1))
                        for k, op in enumerate((ALU.mult, ALU.add)):
                            for g in range(2):
                                rows = slice(g * N, (g + 1) * N)
                                zt = zx[rows, 0, t, :]
                                if k or g:
                                    pool.wait_ge(bn_applied, q.value(8, 4 * t + 2 * k + g))
                                nc.gpsimd.tensor_tensor(zt, zt, tab[rows, k, ds(e[g], 1), :].rearrange("p a d -> p (a d)"),
                                                        op).then_inc(bn_applied, 1)

                    def body(a, b, c):
                        if c is not None:
                            shift(c, 0)
                        if a is not None:
                            if not a.before(1):
                                pool.wait_ge(root1, a.value(1))
                            batch_norm(a, 0)
                        if c is not None:
                            shift(c, 1)
                        if a is not None:
                            batch_norm(a, 1)
                            pool.wait_ge(var1, a.value(1, 1))
                            nc.gpsimd.tensor_tensor(rs1[:], ve1[:], minus_half[:, 0:2], ALU.pow).then_inc(root1, 1)
                        if c is not None:
                            for t in range(2):
                                pool.wait_ge(var2, c.value(2, t + 1))
                                nc.gpsimd.tensor_tensor(rs2[:, t:t + 1], ve2[:, t:t + 1], minus_half[:, 0:1],
                                                        ALU.pow).then_inc(root2, 1)

                    pipeline(pool, body)

                @block.scalar
                def _(act):
                    act.wait_ge(zeros2, 1)

                    def transposed(b, t):
                        act.wait_ge(xT_done, b.value(2, t + 1))
                        if not b.before(1):
                            act.wait_ge(v_done, b.value(2))
                        nc.scalar.activation(xTh[:, :, t * P:(t + 1) * P], ring(RING_XT[t]).rearrange("p (c n) -> p c n", c=C),
                                             ACT.Copy).then_inc(xTh_done, 1)

                    def q_out(b, c_):
                        act.wait_ge(q_done, b.value(C, c_ + 1))
                        if not b.before(2):
                            act.wait_ge(s_done, b.value(2, -2))
                        nc.scalar.activation(
                            qz[b.slot(2)][:, c_, :, :].rearrange("p t (s n) -> p t s n", s=3)[:, :, 0:3:2, :],
                            ring(RING_Q[c_])[:, 0:2 * P].rearrange("p (t g n) -> p t g n", t=2, g=2), ACT.Copy).then_inc(q_set, 1)

                    def k_out(b, c_):
                        act.wait_ge(k_done, b.value(C, c_ + 1))
                        for j in range(HC):
                            rows = slice(j * HD, (j + 1) * HD)
                            ins = nc.scalar.activation(kz[b.slot(2)][rows, c_, :, j * N:(j + 1) * N],
                                                       ring(RING_K[c_])[rows, 0:2 * P].rearrange("p (g n) -> p g n", g=4), ACT.Copy)
                        ins.then_inc(k_set, 1)

                    def v_out(b, t):
                        act.wait_ge(v_done, b.value(2, t + 1))
                        if not b.before(2):
                            act.wait_ge(pv_done, b.value(2, t - 3))
                        for g in range(2):
                            for j in range(2):
                                src = ring(RING_V[t])[g * N:(g + 1) * N, :].rearrange("p (k j d) -> p k j d", j=2, d=HD)[:, :, j, :]
                                ins = nc.scalar.activation(
                                    vz[b.slot(2)][j * N:(j + 1) * N, t, :, g, j * HD:(j + 1) * HD], src, ACT.Copy)
                        ins.then_inc(v_set, 1)

                    def exponential(c, t):
                        act.wait_ge(shifted, c.value(2, t + 1))
                        nc.scalar.activation(sc[:, t, :, :], sc[:, t, :, :], ACT.Exp).then_inc(exp_done, 1)

                    def probs_out(c, t):
                        act.wait_ge(pT_done, c.value(2, t + 1))
                        if not (c.before(1) and t == 0):
                            act.wait_ge(pv_done, c.value(2, t))
                        nc.scalar.activation(pT[:], psT, ACT.Copy).then_inc(pT_set, 1)

                    def o_transposed(c, t):
                        act.wait_ge(oT_done, c.value(2, t + 1))
                        if not c.before(1):
                            act.wait_ge(o_done, c.value(2, t - 1))
                        nc.scalar.activation(oTh[:, t, :, :], ring(RING_OT[t]).rearrange("p (c n) -> p c n", c=C),
                                             ACT.Copy).then_inc(oTh_done, 1)

                    def body(a, b, c):
                        if b is not None:
                            transposed(b, 0)
                            transposed(b, 1)
                        if c is not None:
                            exponential(c, 0)
                        if b is not None:
                            q_out(b, 0)
                            q_out(b, 1)
                        if c is not None:
                            exponential(c, 1)
                        if b is not None:
                            q_out(b, 2)
                            q_out(b, 3)
                            for c_ in range(C):
                                k_out(b, c_)
                        if c is not None:
                            probs_out(c, 0)
                        if b is not None:
                            v_out(b, 0)
                            v_out(b, 1)
                        if c is not None:
                            probs_out(c, 1)
                            o_transposed(c, 0)
                            o_transposed(c, 1)

                    pipeline(act, body)

                @block.vector
                def _(dve):
                    for t_ in (*qz, *kz, *vz):
                        nc.vector.memset(t_[:], 0.0)
                    nc.vector.memset(waiter[:], 0.0).then_inc(zeros2, 1)
                    dve.wait_ge(zeros2, 1)

                    def first_layer(a):
                        slot = a.slot(4)
                        for t in range(2):
                            dve.wait_ge(bn_applied, a.value(8, 4 * t + 4))
                            if not a.before(4):
                                dve.wait_ge(res_done, a.value(2, t - 7))
                            nc.vector.scalar_tensor_tensor(out=x1[:, slot, t, :], in0=zx[:, 0, t, :], scalar=0.0,
                                                           in1=zx[:, 1, t, :], op0=ALU.max, op1=ALU.add).then_inc(relu_res, 1)
                            dve.wait_ge(relu_res, a.value(2, t + 1))
                            nc.vector.bn_stats(st1[:, t, :], x1[:, slot, t, :]).then_inc(stats1, 1)
                            dve.wait_ge(stats1, a.value(2, t + 1))
                            nc.vector.tensor_copy(waiter[:, 0:1], waiter[:, 1:2])
                            nc.vector.bn_aggr(ag1[:, t, :], st1[:, t, :]).then_inc(aggr1, 1)
                        dve.wait_ge(aggr1, a.value(2, 2))
                        nc.vector.tensor_scalar(ve1[:], ag1[:, :, 1], EPS, None, ALU.add).then_inc(var1, 1)

                    def first_norm(a):
                        dve.wait_ge(root1, a.value(1, 1))
                        for t in range(2):
                            xt = x1[:, a.slot(4), t, :]
                            nc.vector.tensor_scalar(xt, xt, ag1[:, t, 0:1], rs1[:, t:t + 1], ALU.subtract, ALU.mult
                                                    ).then_inc(x1_done, 1)

                    def transposed_low(b, t):
                        dve.wait_ge(xTh_done, b.value(2, t + 1))
                        cols = slice(t * P, (t + 1) * P)
                        nc.vector.tensor_tensor(xTl[:, :, cols], ring(RING_XT[t]).rearrange("p (c n) -> p c n", c=C),
                                                xTh[:, :, cols], ALU.subtract).then_inc(xTl_done, 1)

                    def double_adj(c):
                        dve.wait_ge(adj_loaded, c.value(16, 16))
                        if not c.before(1):
                            dve.wait_ge(biased, c.value(2))
                        nc.vector.tensor_tensor(adj2[:], adj_in[:], adj_in[:], ALU.add).then_inc(adj2_done, 1)

                    def add_bias(c, t):
                        dve.wait_ge(s_done, c.value(2, t + 1))
                        if t == 0:
                            dve.wait_ge(adj2_done, c.value(1, 1))
                        if not c.before(1):
                            dve.wait_ge(pT_done, c.value(2, t - 1))
                            dve.wait_ge(tot_done, c.value(2, t - 1))
                        nc.vector.scalar_tensor_tensor(out=sc[:, t, :, :], in0=psS.rearrange("p (h m) -> p h m", m=N), scalar=SCALE,
                                                       in1=adj2[:, t, :].unsqueeze(1).to_broadcast([P, H, N]),
                                                       op0=ALU.mult, op1=ALU.add).then_inc(biased, 1)

                    def maxima(c, t):
                        dve.wait_ge(biased, c.value(2, t + 1))
                        if not c.before(1):
                            dve.wait_ge(shifted, c.value(2, t - 1))
                            dve.wait_ge(inv_done, c.value(2, t - 1))
                        nc.vector.tensor_reduce(mx[:, t, :], sc[:, t, :, :], AX.X, ALU.max).then_inc(max_done, 1)
                        nc.vector.tensor_reduce(amx[:, t, :], sc[:, t, :, :], AX.X, ALU.max,
                                                apply_absolute_value=True).then_inc(absmax_done, 1)

                    def totals(c, t):
                        dve.wait_ge(exp_done, c.value(2, t + 1))
                        if not c.before(1):
                            dve.wait_ge(inv_done, c.value(2, t - 1))
                        nc.vector.tensor_reduce(tot[:, t, :], sc[:, t, :, :], AX.X, ALU.add).then_inc(tot_done, 1)
                        dve.wait_ge(tot_done, c.value(2, t + 1))
                        if not c.before(1):
                            dve.wait_ge(o_normed, c.value(4, 2 * t - 2))
                        nc.vector.reciprocal(inv[:, t, :], tot[:, t, :]).then_inc(tot_inv, 1)
                        dve.wait_ge(tot_inv, c.value(2, t + 1))
                        nc.vector.scalar_tensor_tensor(out=inv[:, t, :], in0=amx[:, t, :], scalar=0.0, in1=inv[:, t, :],
                                                       op0=ALU.is_gt, op1=ALU.mult).then_inc(inv_done, 1)

                    def normalise(c, t):
                        dve.wait_ge(pv_done, c.value(2, t + 1))
                        dve.wait_ge(inv_done, c.value(2, t + 1))
                        if not c.before(1):
                            dve.wait_ge(oT_done, c.value(2, t - 1))
                        for g in range(2):
                            rows = slice(g * N, (g + 1) * N)
                            nc.vector.tensor_tensor(
                                o[rows, t, :].rearrange("p (k j d) -> p k j d", j=2, d=HD),
                                psO[rows, :, g, :].rearrange("p k (j d) -> p k j d", d=HD),
                                inv[rows, t, :].rearrange("p (k j) -> p k j", j=2).unsqueeze(3).to_broadcast([N, H // 2, 2, HD]),
                                ALU.mult).then_inc(o_normed, 1)

                    def o_transposed_low(c, t):
                        dve.wait_ge(oTh_done, c.value(2, t + 1))
                        nc.vector.tensor_tensor(oTl[:, t, :, :], ring(RING_OT[t]).rearrange("p (c n) -> p c n", c=C),
                                                oTh[:, t, :, :], ALU.subtract).then_inc(oTl_done, 1)

                    def second_residual(c, t):
                        dve.wait_ge(o_done, c.value(2, t + 1))
                        if not c.before(1):
                            dve.wait_ge(out_stored[t], c.value(16))
                        nc.vector.tensor_tensor(res[:, t, :], ring(RING_O[t]), x1[:, c.slot(4), t, :], ALU.add).then_inc(res_done, 1)
                        dve.wait_ge(res_done, c.value(2, t + 1))
                        nc.vector.bn_stats(st2[:, t, :], res[:, t, :]).then_inc(stats2, 1)
                        dve.wait_ge(stats2, c.value(2, t + 1))
                        nc.vector.tensor_copy(waiter[:, 0:1], waiter[:, 1:2])
                        nc.vector.bn_aggr(ag2[:, t, :], st2[:, t, :]).then_inc(aggr2, 1)
                        dve.wait_ge(aggr2, c.value(2, t + 1))
                        nc.vector.tensor_scalar(ve2[:, t:t + 1], ag2[:, t, 1:2], EPS, None, ALU.add).then_inc(var2, 1)

                    def second_norm(c, t):
                        dve.wait_ge(root2, c.value(2, t + 1))
                        nc.vector.tensor_scalar(res[:, t, :], res[:, t, :], ag2[:, t, 0:1], rs2[:, t:t + 1],
                                                ALU.subtract, ALU.mult).then_inc(out_done, 1)

                    def body(a, b, c):
                        if c is not None:
                            double_adj(c)
                            add_bias(c, 0)
                        if b is not None:
                            transposed_low(b, 0)
                            transposed_low(b, 1)
                        if c is not None:
                            maxima(c, 0)
                            add_bias(c, 1)
                            maxima(c, 1)
                        if a is not None:
                            first_layer(a)
                        if c is not None:
                            totals(c, 0)
                            totals(c, 1)
                        if a is not None:
                            first_norm(a)
                        if c is not None:
                            normalise(c, 0)
                            o_transposed_low(c, 0)
                            normalise(c, 1)
                            second_residual(c, 0)
                            o_transposed_low(c, 1)
                            second_norm(c, 0)
                            second_residual(c, 1)
                            second_norm(c, 1)

                    pipeline(dve, body)

                @block.tensor
                def _(pe):
                    def split_product(dst, lhs_h, lhs_l, rhs_h, rhs_l):
                        n = 0
                        for lhs, rhs in ((lhs_h, rhs_h), (lhs_h, rhs_l), (lhs_l, rhs_h)):
                            for c_ in range(C):
                                ins = pe.matmul(dst, lhs(c_), rhs(c_), start=(n == 0), stop=(n == NT * C - 1))
                                n += 1
                        return ins

                    def transposes(b, t):
                        pe.wait_ge(x1_done, b.value(2, t + 1))
                        if not b.before(2):
                            pe.wait_ge((oTl_done, res_done)[t], b.value(2, -3))
                        elif not b.before(1):
                            pe.wait_ge(k_set, C)
                        for c_ in range(C):
                            ins = pe.transpose(ring(RING_XT[t])[:, c_ * P:(c_ + 1) * P],
                                               x1[:, b.slot(4), t, c_ * P:(c_ + 1) * P], ident[:])
                        ins.then_inc(xT_done, 1)

                    def scores(c, t):
                        if t == 0:
                            pe.wait_ge(q_set, c.value(C, C))
                            pe.wait_ge(k_set, c.value(C, C))
                            if not c.before(1):
                                pe.wait_ge(o_normed, c.value(4))
                        else:
                            pe.wait_ge(biased, c.value(2, 1))
                        p = c.slot(2)
                        for c_ in range(C):
                            for g in range(2):
                                ins = pe.matmul(psS[:, c_ * HC * N:(c_ + 1) * HC * N], qz[p][:, c_, t, g * N:g * N + P],
                                                kz[p][:, c_, 2 * t + g, :], start=(g == 0), stop=(g == 1))
                        ins.then_inc(s_done, 1)

                    def project(b, w, c_, uses, done, free, value):
                        pe.wait_ge(free, value)
                        cols = slice(c_ * P, (c_ + 1) * P)
                        split_product(ring(uses[c_])[:, 0:2 * P], lambda i: wp_h[:, w, i, cols], lambda i: wp_l[:, w, i, cols],
                                      lambda i: xTh[:, i, :], lambda i: xTl[:, i, :]).then_inc(done, 1)

                    def values(b, t):
                        pe.wait_ge(k_set, b.value(C, t + 1))
                        cols = slice(t * P, (t + 1) * P)
                        split_product(ring(RING_V[t]), lambda i: xTh[:, i, cols], lambda i: xTl[:, i, cols],
                                      lambda i: wp_h[:, 2, i, :], lambda i: wp_l[:, 2, i, :]).then_inc(v_done, 1)

                    def prob_transposes(c, t):
                        pe.wait_ge(exp_done, c.value(2, t + 1))
                        if not (c.before(1) and t == 0):
                            pe.wait_ge(pT_set, c.value(2, t))
                        for k in range(H // 2):
                            ins = pe.transpose(psT[:, k, :], sc[:, t, 2 * k:2 * k + 2, :].rearrange("p h m -> p (h m)"), ident[:])
                        ins.then_inc(pT_done, 1)

                    def attend(c, t):
                        pe.wait_ge(pT_set, c.value(2, t + 1))
                        pe.wait_ge(v_set, c.value(2, t + 1))
                        if t == 0:
                            pe.wait_ge(biased, c.value(2, 2))
                        else:
                            pe.wait_ge(o_normed, c.value(4, 2))
                        for k in range(H // 2):
                            ins = pe.matmul(psO[:, k, :, :].rearrange("p g n -> p (g n)"), pT[:, k, :],
                                            vz[c.slot(2)][:, t, k, :, :].rearrange("p g n -> p (g n)"), start=True, stop=True)
                        ins.then_inc(pv_done, 1)

                    def o_transposes(c, t, last):
                        pe.wait_ge(o_normed, c.value(4, 2 * t + 2))
                        pe.wait_ge(*last)
                        for c_ in range(C):
                            ins = pe.transpose(ring(RING_OT[t])[:, c_ * P:(c_ + 1) * P], o[:, t, c_ * P:(c_ + 1) * P], ident[:])
                        ins.then_inc(oT_done, 1)

                    def output(c, t, last):
                        pe.wait_ge(oTl_done, c.value(2, t + 1))
                        pe.wait_ge(*last)
                        split_product(ring(RING_O[t]), lambda i: oTh[:, t, i, :], lambda i: oTl[:, t, i, :],
                                      lambda i: wp_h[:, 3, i, :], lambda i: wp_l[:, 3, i, :]).then_inc(o_done, 1)

                    def body(a, b, c):
                        if c is not None:
                            scores(c, 0)
                        if b is not None:
                            transposes(b, 0)
                            transposes(b, 1)
                        if c is not None:
                            scores(c, 1)
                        if b is not None:
                            pe.wait_ge(xTl_done, b.value(2, 2))
                            for c_ in range(C):
                                if c_ == 0 and not b.before(2):
                                    pe.wait_ge(oTl_done, b.value(2, -2))
                                    pe.wait_ge(res_done, b.value(2, -2))
                                elif c_ == 0 and not b.before(1):
                                    pe.wait_ge(v_set, 2)
                                project(b, 0, c_, RING_Q, q_done, xTl_done, b.value(2, 2))
                            for c_ in range(C):
                                project(b, 1, c_, RING_K, k_done, q_set, b.value(C, c_ + 1))
                        if c is not None:
                            prob_transposes(c, 0)
                        if b is not None:
                            values(b, 0)
                        if c is not None:
                            attend(c, 0)
                        if b is not None:
                            values(b, 1)
                        if c is not None:
                            prob_transposes(c, 1)
                            if b is not None:
                                last = ((k_set, b.value(C, 3)), (k_set, b.value(C, 4)), (v_set, b.value(2, 1)), (v_set, b.value(2, 2)))
                            else:
                                last = ((oTl_done, c.value(2, -1)), (res_done, c.value(2, -1)),
                                        (oTl_done, c.value(2)), (res_done, c.value(2)))
                            o_transposes(c, 0, last[0])
                            attend(c, 1)
                            output(c, 0, last[1])
                            o_transposes(c, 1, last[2])
                            output(c, 1, last[3])

                    pipeline(pe, body)


_IN = ["x", "adj", "adjT", "router_w", "router_b", "expert_w", "gamma", "beta", "wqT", "wkT", "wvT", "woT"]


def kernel(x, adj, L0_gnn_router_w, L0_gnn_router_b, L0_gnn_expert_w, L0_gnn_bn_gamma, L0_gnn_bn_beta,
           L1_gnn_Wq, L1_gnn_Wk, L1_gnn_Wv, L1_gnn_Wo):
    import concourse.bacc as bacc
    from concourse.bass_utils import run_bass_kernel_spmd

    laid_out = dict(
        x=x, adj=adj, adjT=np.swapaxes(adj, 1, 2), router_w=L0_gnn_router_w, router_b=L0_gnn_router_b,
        expert_w=L0_gnn_expert_w, gamma=L0_gnn_bn_gamma, beta=L0_gnn_bn_beta,
        wqT=np.swapaxes(L1_gnn_Wq, 0, 1), wkT=np.swapaxes(L1_gnn_Wk, 0, 1),
        wvT=np.swapaxes(L1_gnn_Wv, 0, 1), woT=np.swapaxes(L1_gnn_Wo, 0, 1),
    )
    nc = bacc.Bacc("TRN2", target_bir_lowering=False, num_devices=1)
    arrays, args = {}, []
    for name in _IN:
        a = np.ascontiguousarray(laid_out[name])
        arrays[f"in_{name}"] = a
        args.append(nc.dram_tensor(f"in_{name}", a.shape, mybir.dt.from_np(a.dtype), kind="ExternalInput").ap())
    args.append(nc.dram_tensor("out_0", x.shape, F32, kind="ExternalOutput").ap())
    graph_layers(nc, *args)
    r = run_bass_kernel_spmd(nc, [arrays], core_ids=[0])
    return r.results[0]["out_0"]
```

```python
from contextlib import ExitStack

import numpy as np

import concourse.bass as bass
from concourse import mybir
from concourse.bass import ds

F32 = mybir.dt.float32
F32R = mybir.dt.float32r
I32 = mybir.dt.int32
ALU = mybir.AluOpType
ACT = mybir.ActivationFunctionType
AX = mybir.AxisListType

P = 128
RING1 = 4
RINGZ = 4
EPS = 1e-5


class Number:

    def __init__(self, k, i=None, unroll=1):
        self.k, self.i, self.unroll = k, i, unroll

    def __add__(self, n):
        return Number(self.k + n, self.i, self.unroll)

    def value(self, per_quad, extra=0):
        if self.i is None:
            return per_quad * self.k + extra
        return self.i * (per_quad * self.unroll) + (per_quad * self.k + extra)

    def turn(self, n, per_turn, extra=0):
        if self.i is None:
            return per_turn * (self.k // n) + extra
        return self.i * (per_turn * (self.unroll // n)) + (per_turn * (self.k // n) + extra)

    def slot(self, n):
        return self.k % n

    def half(self):
        return Number(self.k // 2, self.i, self.unroll // 2)

    def before(self, n):
        return self.i is None and self.k < n


def steps(eng, body, first, loop_from, loop_to, last, unroll):
    for s in range(first, loop_from):
        body(Number(s))
    assert (loop_to - loop_from) % unroll == 0
    if loop_to > loop_from:
        with eng.Fori(0, (loop_to - loop_from) // unroll) as i:
            for u in range(unroll):
                body(Number(loop_from + u, i, unroll))
    for s in range(loop_to, last + 1):
        body(Number(s))


def graph_layers(nc, x, adj, adjT, router_w, router_b, expert_w, gammaT, betaT, wqT, wkT, wvT, woT, out):
    B, N, D = x.shape
    E = expert_w.shape[0]
    H = 16
    HD = D // H
    C = D // P
    HC = P // HD
    NQ = B // 4
    SLOTS = B + E
    TILES = SLOTS // 2
    YG = C * N
    BIG = max(B + 1, P + 1) * YG
    SCALE = float(D) ** -0.5
    assert 2 * N == P and D == 512 and E == 4 and B <= P and SLOTS % 4 == 0

    x_q = x.rearrange("(q t g) n d -> q (g n) t d", t=2, g=2)
    out_q = out.rearrange("(q t g) n d -> q t (g n) d", t=2, g=2)
    adj_q = adj.rearrange("(q t g) n m -> q (g n) t m", t=2, g=2)
    adjT_pairs = adjT.rearrange("(q t g) m n -> q g m t n", t=4, g=2)

    z_dram = nc.dram_tensor("z_scratch", [B + SLOTS, N, D], F32, kind="Internal").ap()
    z_q = z_dram[0:B].rearrange("(q t g) n d -> q (g n) t d", t=2, g=2)

    outer = ExitStack()
    with outer:
        def sem(name):
            return outer.enter_context(nc.semaphore(name))

        ps = outer.enter_context(nc.psum_tensor("ps", [P, 8, 512], F32))

        def sb(stack, name, shape, dt=F32):
            return stack.enter_context(nc.sbuf_tensor(name, shape, dt))

        w_h = sb(outer, "w_h", [P, 4, C, D], F32R)
        w_l = sb(outer, "w_l", [P, 4, C, D], F32R)
        big = sb(outer, "big", [P, BIG])
        ident = sb(outer, "ident", [P, P])
        expert = sb(outer, "expert", [1, B], I32)
        minus_half = sb(outer, "minus_half", [P, C * E])

        used = [0]

        def part(*shape):
            n = int(np.prod(shape))
            at = used[0]
            used[0] += n
            assert used[0] <= BIG
            names = "abcde"[:len(shape)]
            return big[:, at:at + n].rearrange(f"p ({' '.join(names)}) -> p {' '.join(names)}", **dict(zip(names, shape)))

        tab = part(2, E, D)
        kz = [part(C, 4, HC * N) for p in range(2)]
        vz = [part(2, H // 2, 2, 2 * HD) for p in range(2)]
        zx = part(2, 2, D)
        passing = used[0]
        raw2 = part(4, C, D)
        square_sums = part(E, D)
        rows = part(2, D)
        used[0] = passing

        zx_loaded = sem("zx_loaded")

        def load_zx(sp, q):
            row = ds(q.value(1), 1)
            sp.dma_start(zx[:, 0, :, :], z_q[row].rearrange("a p t d -> (a p) t d")).then_inc(zx_loaded, 16)
            sp.dma_start(zx[:, 1, :, :], x_q[row].rearrange("a p t d -> (a p) t d")).then_inc(zx_loaded, 16)

        with ExitStack() as st:
            x_in = [big[:, (NQ - RING1 + m) * 4 * YG:(NQ - RING1 + m + 1) * 4 * YG].rearrange("p (t d) -> p t d", t=2)
                    for m in range(RING1)]
            z_sums = sb(st, "z_sums", [P, E, D])
            raw = z_sums[:, 0:2, :]
            zs = sb(st, "zs", [P, RINGZ, D])
            square = sb(st, "square", [P, D])
            early = zs[:].rearrange("p t d -> p (t d)")
            aT = early[:, 0:RING1 * 2 * (P + 2)].rearrange("p (m t n) -> p m t n", m=RING1, t=2)
            xsum = early[:, RINGZ * D - C * B:].rearrange("p (c b) -> p c b", c=C)
            assert RING1 * 2 * (P + 2) + B + SLOTS + C * B <= RINGZ * D
            yh = sb(st, "yh", [P, 2, C, P], F32R)
            yl = sb(st, "yl", [P, 2, C, P], F32R)
            rw = sb(st, "rw", [P, C, E])
            rb = sb(st, "rb", [B, E])
            gT = sb(st, "gT", [P, C, E])
            bT = sb(st, "bT", [P, C, E])
            ones = sb(st, "ones", [P, 1])
            minus_eid = sb(st, "minus_eid", [P, E])
            slot_id_i = sb(st, "slot_id_i", [P, SLOTS], I32)
            graph_id_i = sb(st, "graph_id_i", [P, 1], I32)
            graph_id = sb(st, "graph_id", [P, 2])
            score = sb(st, "score", [B, E])
            best = sb(st, "best", [B, 1])
            hit = sb(st, "hit", [B, E])
            ecol = sb(st, "ecol", [B, 3])
            onehot = sb(st, "onehot", [B, E])
            rank = sb(st, "rank", [B, 3])
            even_i = sb(st, "even_i", [B, E], I32)
            even = sb(st, "even", [B, E])
            at = RING1 * 2 * (P + 2)
            before = early[0:B, at:at + B]
            slot_id = early[:, at + B:at + B + SLOTS]
            slot_of = early[0:B, 0:SLOTS]
            same = early[0:B, SLOTS:SLOTS + B]
            empty = early[0:1, SLOTS + B:2 * SLOTS + B]
            tile_word = sb(st, "tile_word", [1, TILES], I32)
            place = sb(st, "place", [1, SLOTS], I32)
            tile_expert = sb(st, "tile_expert", [1, TILES], I32)
            inv_count = sb(st, "inv_count", [P, 2, E])
            bn = sb(st, "bn", [P, 4, C, E])

            psY = [ps[:, 2 * m:2 * m + 2, :].rearrange("p b (c n) -> p (b c) n", c=2) for m in range(4)]
            psZ = [ps[:, t, :] for t in range(2)]
            psT1 = [ps[:, 2 + k, :].rearrange("p (c e r) -> p c e r", c=C, e=E) for k in range(2)]
            psTab = [ps[:, bank, :] for bank in (4, 5, 6, 7, 0, 1)]
            psRow = ps[:, 2, :]
            psSmall = ps[:, 3, :]
            psSum = ps[:, 4:8, :]

            w_loaded = [sem(f"w_loaded{p}") for p in range(2)]
            w_high = sem("w_high")
            w_low = sem("w_low")
            small_loaded = sem("small_loaded")
            x_loaded = [sem(f"x_loaded{m}") for m in range(RING1)]
            aT_loaded = [sem(f"aT_loaded{m}") for m in range(RING1 // 2)]
            aT_ready = sem("aT_ready")
            consts1 = sem("consts1")
            ids = sem("ids")
            y_done = sem("y_done")
            y_kept = [sem(f"y_kept{t}") for t in range(2)]
            scored = sem("scored")
            route = sem("route")
            route_pe = sem("route_pe")
            sorted_ = sem("sorted")
            yh_done = sem("yh_done")
            yl_done = sem("yl_done")
            z_done = sem("z_done")
            z_copied = sem("z_copied")
            z_squared = sem("z_squared")
            z_sums_zeroed = sem("z_sums_zeroed")
            square_sums_zeroed = sem("square_sums_zeroed")
            z_summed = sem("z_summed")
            squares_summed = sem("squares_summed")
            z_stored = [sem(f"z_stored{m}") for m in range(RINGZ)]
            zeroed = sem("zeroed")
            raw2_loaded = [sem(f"raw2_loaded{m}") for m in range(4)]
            proj_high = sem("proj_high")
            proj_low = sem("proj_low")
            sums_set = sem("sums_set")
            rows_done = sem("rows_done")
            rows_set = sem("rows_set")
            turned = sem("turned")
            bn_step = sem("bn_step")
            bn_root = sem("bn_root")
            spread = sem("spread")
            tab_set = sem("tab_set")

            NJ = TILES // 2
            w_rows = expert_w.rearrange("e (c p) d -> (e c) p d", p=P)
            wh_c, wl_c = (w.rearrange("p e c d -> p (e c) d") for w in (w_h, w_l))
            NW = E * C
            PIECES = min(NW, NQ // 2)
            assert NQ % 4 == 0

            def graph_cols(q, t):
                return big[:, ds(q.value(4 * YG, 2 * t * YG), 2 * YG)].rearrange("p (g c n) -> p c g n", g=2, c=C)

            def keep_y(eng, op, q, t):
                eng.wait_ge(y_done, q.value(2, t + 1))
                src = psY[2 * q.slot(2) + t]
                op(xsum[:, :, ds(q.value(4, 2 * t), 2)], src[:, :, P:P + 2]).then_inc(y_kept[t], 1)
                op(graph_cols(q, t), src[:, :, 0:P].rearrange("p c (g n) -> p c g n", g=2)).then_inc(y_kept[t], 1)

            def act_copy(dst, src):
                return nc.scalar.activation(dst, src, ACT.Copy)

            def with_pieces(keep, split):
                def step(q):
                    keep(q)
                    if q.slot(2) == 1 and (q.i is not None or q.k // 2 < NW):
                        split(q.half())
                return step

            def row(tensor, reg):
                return tensor[:, ds(reg, 1), :].rearrange("p a d -> p (a d)")

            def expert_of(eng, j, t):
                return eng.value_load(tile_expert[0:1, ds(j.value(2, t), 1)], min_val=0, max_val=E - 1)

            def z_slot(j, t):
                return 2 * j.slot(2) + t

            def y_half(g):
                return big[:, ds(g * YG, YG)].rearrange("p (c n) -> p c n", c=C)

            def word_of(eng, j, t):
                return eng.value_load(tile_word[0:1, ds(j.value(2, t), 1)], min_val=0, max_val=B * 257 + (E - 1) * 65536)

            def graphs_in(word):
                return [nc.s_assert_within(g % 256, 0, B, skip_runtime_bounds_check_because="a graph's number or B was packed")
                        for g in (word, word // 256)]

            with nc.Block() as block:

                @block.sync
                def _(sp):
                    def load_x(q):
                        p = q.slot(RING1)
                        sp.dma_start(x_in[p], x_q[ds(q.value(1), 1)].rearrange("a p t d -> (a p) t d")).then_inc(x_loaded[p], 16)

                    def load_adj(q):
                        p = q.slot(RING1)
                        for g in range(2):
                            sp.dma_start(aT[g * N:(g + 1) * N, p:p + 2, :, g * N:(g + 1) * N].rearrange("m q t n -> m (q t) n"),
                                         adjT_pairs[ds(q.half().value(1), 1), g].rearrange("a m t n -> (a m) t n")
                                         ).then_inc(aT_loaded[p // 2], 16)

                    def load_weights(n):
                        if not n.before(2):
                            sp.wait_ge(w_low, n.value(1, -1))
                        sp.dma_start(raw[:, n.slot(2), :], w_rows[ds(n.value(1), 1)].rearrange("a p d -> (a p) d")
                                     ).then_inc(w_loaded[n.slot(2)], 16)

                    for q in range(RING1):
                        load_x(Number(q))
                        if q == 0:
                            sp.wait_ge(aT_ready, 1)
                        if q % 2 == 0:
                            load_adj(Number(q))
                        if 0 < q < 3:
                            load_weights(Number(q - 1))
                    sp.dma_start(rw[:], router_w.rearrange("(c p) e -> p c e", p=P)).then_inc(small_loaded, 16)
                    sp.dma_start(rb[:], router_b.rearrange("(a e) -> a e", a=1).to_broadcast([B, E])).then_inc(small_loaded, 16)
                    sp.dma_start(gT[:], gammaT.rearrange("(c p) e -> p c e", p=P)).then_inc(small_loaded, 16)
                    sp.dma_start(bT[:], betaT.rearrange("(c p) e -> p c e", p=P)).then_inc(small_loaded, 16)

                    def step(q):
                        sp.wait_ge(y_done, q.value(2, 2))
                        load_x(q + RING1)
                        if q.slot(2) == 1:
                            load_adj(q + (RING1 - 1))
                            load_weights(q.half() + 2)

                    steps(sp, step, 0, 0, NQ - RING1, NQ - RING1 - 1, RING1)
                    for n in range(PIECES, NW):
                        load_weights(Number(n))

                    sp.wait_ge(sorted_, 4)

                    def store(j):
                        for t in range(2):
                            g = [sp.value_load(place[0:1, ds(j.value(4, 2 * t + h), 1)], min_val=0, max_val=B + SLOTS - 1)
                                 for h in range(2)]
                            sp.wait_ge(z_copied, j.value(2, t + 1))
                            for h in range(2):
                                sp.dma_start(z_dram[ds(g[h], 1)].rearrange("a n d -> (a n) d"),
                                             zs[h * N:(h + 1) * N, z_slot(j, t), :]).then_inc(z_stored[z_slot(j, t)], 16)

                    steps(sp, store, 0, 3, NJ - 2, NJ - 2, 2)
                    sp.wait_ge(yl_done, 4 * NJ)
                    sp.wait_ge(yh_done, 4 * NJ)
                    for m, w in enumerate((wqT, wkT, wvT, woT)):
                        sp.dma_start(raw2[:, m, :, :], w.rearrange("(c p) d -> p c d", p=P)).then_inc(raw2_loaded[m], 16)
                    store(Number(NJ - 1))
                    for m in range(RINGZ):
                        sp.wait_ge(z_stored[m], 32 * ((TILES - m + RINGZ - 1) // RINGZ))
                    load_zx(sp, Number(0))

                @block.gpsimd
                def _(pool):
                    nc.gpsimd.memset(ident[:], 0.0).then_inc(ids, 1)
                    nc.gpsimd.memset(before, 0.0).then_inc(ids, 1)
                    nc.gpsimd.iota(slot_id_i[:], pattern=[[1, SLOTS]], base=0, channel_multiplier=0).then_inc(ids, 1)
                    nc.gpsimd.iota(graph_id_i[:], pattern=[[0, 1]], base=-B, channel_multiplier=1).then_inc(ids, 1)
                    pool.wait_ge(ids, 4)
                    nc.gpsimd.affine_select(out=ident[:], in_=ident[:], compare_op=ALU.not_equal, fill=1.0,
                                            base=0, pattern=[[-1, P]], channel_multiplier=1).then_inc(ids, 1)
                    nc.gpsimd.affine_select(out=before, in_=before, compare_op=ALU.is_ge, fill=1.0,
                                            base=0, pattern=[[1, B]], channel_multiplier=-1).then_inc(ids, 1)
                    nc.gpsimd.memset(minus_half[:], -0.5).then_inc(ids, 1)
                    pool.wait_ge(w_low, NW)
                    nc.gpsimd.memset(z_sums[:], 0.0).then_inc(z_sums_zeroed, 1)
                    pool.wait_ge(sorted_, 4)
                    pool.wait_ge(z_sums_zeroed, 1)

                    def add_z(j):
                        for t in range(2):
                            e = expert_of(pool, j, t)
                            pool.wait_ge(z_copied, j.value(2, t + 1))
                            if not (j.before(1) and t == 0):
                                pool.wait_ge(z_summed, j.value(2, t))
                            sums = row(z_sums, e)
                            nc.gpsimd.tensor_tensor(sums, sums, zs[:, z_slot(j, t), :], ALU.add).then_inc(z_summed, 1)

                    steps(pool, add_z, 0, 3, NJ, NJ - 1, 2)
                    pool.wait_ge(yl_done, 4 * NJ)
                    pool.wait_ge(yh_done, 4 * NJ)
                    nc.gpsimd.memset(kz[0], 0.0).then_inc(zeroed, 1)
                    pool.wait_ge(bn_step, 3)
                    pool.wait_ge(ids, 7)
                    nc.gpsimd.tensor_tensor(bn[:, 1, :, :], bn[:, 1, :, :],
                                            minus_half[:].rearrange("p (c e) -> p c e", c=C), ALU.pow).then_inc(bn_root, 1)
                    for zeros in (kz[1], *vz):
                        nc.gpsimd.memset(zeros, 0.0).then_inc(zeroed, 1)
                    pool.wait_ge(zeroed, 4)

                @block.scalar
                def _(act):
                    def keep(q):
                        keep_y(act, act_copy, q, 0)

                    def high_part(n):
                        act.wait_ge(w_loaded[n.slot(2)], n.turn(2, 16, 16))
                        act_copy(row(wh_c, n.value(1)), raw[:, n.slot(2), :]).then_inc(w_high, 1)

                    steps(act, with_pieces(keep, high_part), 0, 0, NQ, NQ - 1, 4)
                    for n in range(PIECES, NW):
                        high_part(Number(n))

                    act.wait_ge(sorted_, 4)
                    for t in range(2):
                        act.wait_ge(y_kept[t], 2 * NQ)

                    def y_high(j, t):
                        g = graphs_in(word_of(act, j, t))
                        if not j.before(1):
                            act.wait_ge(z_done, j.value(2, t - 1))
                        for h in range(2):
                            act_copy(yh[:, t, :, h * N:(h + 1) * N], y_half(g[h])).then_inc(yh_done, 1)

                    def z_out(j, t):
                        act.wait_ge(z_done, j.value(2, t + 1))
                        if not j.before(2):
                            act.wait_ge(z_stored[z_slot(j, t)], j.turn(2, 32))
                            act.wait_ge(z_summed, j.value(2, t - 3))
                        act_copy(zs[:, z_slot(j, t), :], psZ[t]).then_inc(z_copied, 1)
                        act.wait_ge(z_copied, j.value(2, t + 1))
                        if not (j.before(1) and t == 0):
                            act.wait_ge(squares_summed, j.value(2, t))
                        nc.scalar.activation(square[:], zs[:, z_slot(j, t), :], ACT.Square).then_inc(z_squared, 1)

                    def step(j):
                        for t in range(2):
                            y_high(j, t)
                            if not j.before(1):
                                z_out(j + -1, t)

                    steps(act, step, 0, 3, NJ, NJ - 1, 2)
                    for t in range(2):
                        z_out(Number(NJ - 1), t)

                    act.wait_ge(squares_summed, TILES)
                    act_copy(square_sums[:, 0:2, :], psSum[:, 0:2, :]).then_inc(sums_set, 1)

                    def proj_high_part(m):
                        act.wait_ge(raw2_loaded[m], 16)
                        act_copy(w_h[:, m, :, :], raw2[:, m, :, :]).then_inc(proj_high, 1)

                    act.wait_ge(z_done, TILES)
                    act.wait_ge(rows_done, 1)
                    act_copy(rows[:, 0, :], ps[:, 0, :]).then_inc(rows_set, 1)
                    for m in range(4):
                        proj_high_part(m)
                    for k in range(2):
                        for e in range(E):
                            act.wait_ge(spread, k * E + e + 1)
                            act_copy(tab[:, k, e, :], psTab[(k * E + e) % 6]).then_inc(tab_set, 1)

                @block.vector
                def _(dve):
                    nc.vector.memset(aT, 0.0).then_inc(consts1, 1)
                    dve.wait_ge(consts1, 1)
                    for g in range(2):
                        ins = nc.vector.memset(aT[g * N:(g + 1) * N, :, :, P + g:P + g + 1], 1.0)
                    ins.then_inc(aT_ready, 1)
                    nc.vector.memset(ones[:], 1.0)
                    for e in range(E):
                        nc.vector.memset(minus_eid[:, e:e + 1], float(e - E))
                    nc.vector.memset(big[:, B * YG:(B + 1) * YG], 0.0).then_inc(consts1, 1)

                    def expert_low_part(n):
                        dve.wait_ge(w_high, n.value(1, 1))
                        nc.vector.tensor_tensor(row(wl_c, n.value(1)), raw[:, n.slot(2), :], row(wh_c, n.value(1)),
                                                ALU.subtract).then_inc(w_low, 1)

                    keep = with_pieces(lambda q: keep_y(dve, nc.vector.tensor_copy, q, 1), expert_low_part)
                    steps(dve, keep, 0, 0, NQ, NQ - 1, 4)
                    for n in range(PIECES, NW):
                        expert_low_part(Number(n))

                    chain = [0]

                    def link(ins):
                        chain[0] += 1
                        ins.then_inc(route, 1)
                        dve.wait_ge(route, chain[0])

                    dve.wait_ge(ids, 7)
                    dve.wait_ge(consts1, 2)
                    dve.wait_ge(small_loaded, 64)
                    nc.vector.tensor_copy(slot_id, slot_id_i[:])
                    nc.vector.tensor_copy(graph_id[:, 0:1], graph_id_i[:])
                    nc.vector.tensor_scalar(graph_id[:, 1:2], graph_id_i[:], 256.0, None, ALU.mult)
                    dve.wait_ge(scored, 1)
                    link(nc.vector.scalar_tensor_tensor(out=score[:], in0=psSmall[0:B, 0:E], scalar=1.0 / N, in1=rb[:],
                                                        op0=ALU.mult, op1=ALU.add))
                    link(nc.vector.tensor_reduce(best[:], score[:], AX.X, ALU.max))
                    link(nc.vector.scalar_tensor_tensor(out=hit[:], in0=score[:], scalar=best[:, 0:1], in1=minus_eid[0:B, :],
                                                        op0=ALU.is_ge, op1=ALU.mult))
                    link(nc.vector.tensor_reduce(ecol[:, 0:1], hit[:], AX.X, ALU.min))
                    nc.vector.tensor_scalar(ecol[:, 1:2], ecol[:, 0:1], float(E), None, ALU.add)
                    nc.vector.tensor_scalar(ecol[:, 2:3], ecol[:, 0:1], float(E), 65536.0, ALU.add, ALU.mult)
                    link(nc.vector.tensor_scalar(onehot[:], minus_eid[0:B, :], ecol[:, 0:1], None, ALU.is_equal))
                    for t in range(2):
                        dve.wait_ge(y_kept[t], 2 * NQ)
                    nc.vector.memset(psSum[:, 0:2, :], 0.0).then_inc(square_sums_zeroed, 1)
                    dve.wait_ge(route_pe, 1)
                    nc.vector.tensor_copy(expert[:], psRow[0:1, 0:B]).then_inc(sorted_, 1)
                    link(nc.vector.scalar_tensor_tensor(out=same, in0=psRow[0:B, 0:B], scalar=ecol[:, 1:2], in1=before,
                                                        op0=ALU.is_equal, op1=ALU.mult))
                    link(nc.vector.tensor_reduce(rank[:, 0:1], same, AX.X, ALU.add))
                    link(nc.vector.tensor_scalar(even_i[:], psRow[0:B, B:B + E], 1.0, None, ALU.add))
                    link(nc.vector.tensor_scalar(even_i[:], even_i[:], 1, 1, ALU.logical_shift_right, ALU.logical_shift_left))
                    link(nc.vector.tensor_copy(even[:], even_i[:]))
                    link(nc.vector.scalar_tensor_tensor(out=even[:], in0=minus_eid[0:B, :], scalar=ecol[:, 0:1], in1=even[:],
                                                        op0=ALU.is_lt, op1=ALU.mult))
                    link(nc.vector.tensor_reduce(rank[:, 1:2], even[:], AX.X, ALU.add))
                    link(nc.vector.tensor_tensor(rank[:, 2:3], rank[:, 0:1], rank[:, 1:2], ALU.add))
                    link(nc.vector.tensor_scalar(slot_of, slot_id[0:B, :], rank[:, 2:3], None, ALU.is_equal))
                    link(nc.vector.tensor_scalar(inv_count[:, 0, :], psRow[:, B:B + E], float(N), 1.0, ALU.mult, ALU.max))
                    link(nc.vector.reciprocal(inv_count[:, 1, :], inv_count[:, 0, :]))
                    nc.vector.memset(psSum[:, 2:4, :], 0.0).then_inc(square_sums_zeroed, 1)
                    dve.wait_ge(route_pe, 2)
                    nc.vector.tensor_scalar(tile_word[:], psSmall[0:1, SLOTS + TILES:SLOTS + 2 * TILES], float(B * 257), None,
                                            ALU.add).then_inc(sorted_, 1)
                    link(nc.vector.tensor_scalar(empty, slot_id[0:1, :], float(B), None, ALU.add))
                    link(nc.vector.scalar_tensor_tensor(out=empty, in0=psSmall[0:1, 0:SLOTS], scalar=0.0, in1=empty,
                                                        op0=ALU.is_equal, op1=ALU.mult))
                    nc.vector.scalar_tensor_tensor(out=place[:], in0=psSmall[0:1, 0:SLOTS], scalar=float(B), in1=empty,
                                                   op0=ALU.add, op1=ALU.max).then_inc(sorted_, 1)
                    nc.vector.tensor_copy(tile_expert[:], psSmall[0:1, SLOTS:SLOTS + TILES]).then_inc(sorted_, 1)
                    dve.wait_ge(sorted_, 4)
                    dve.wait_ge(square_sums_zeroed, 2)

                    def y_low(j, t):
                        word = word_of(dve, j, t)
                        g = graphs_in(word)
                        for h in range(2):
                            dve.wait_ge(yh_done, j.value(4, 2 * t + h + 1))
                            half = slice(h * N, (h + 1) * N)
                            nc.vector.tensor_tensor(yl[:, t, :, half], y_half(g[h]), yh[:, t, :, half], ALU.subtract).then_inc(yl_done, 1)
                        return word // 65536

                    def add_squares(j, t, e):
                        dve.wait_ge(z_squared, j.value(2, t + 1))
                        if not (j.before(1) and t == 0):
                            dve.wait_ge(squares_summed, j.value(2, t))
                        sums = row(psSum, e)
                        nc.vector.tensor_tensor(sums, sums, square[:], ALU.add).then_inc(squares_summed, 1)

                    def step(j):
                        for t in range(2):
                            e = y_low(j, t)
                            if not j.before(1):
                                add_squares(j + -1, t, e)

                    steps(dve, step, 0, 3, NJ, NJ - 1, 2)
                    for t in range(2):
                        add_squares(Number(NJ - 1), t, expert_of(dve, Number(NJ - 1), t))
                    dve.wait_ge(squares_summed, TILES)
                    nc.vector.tensor_copy(square_sums[:, 2:4, :], psSum[:, 2:4, :]).then_inc(sums_set, 1)

                    at = [0]

                    def bn_link(ins):
                        at[0] += 1
                        ins.then_inc(bn_step, 1)
                        dve.wait_ge(bn_step, at[0])

                    def low_part(m):
                        dve.wait_ge(proj_high, m + 1)
                        nc.vector.tensor_tensor(w_l[:, m, :, :], raw2[:, m, :, :], w_h[:, m, :, :], ALU.subtract).then_inc(proj_low, 1)

                    dve.wait_ge(rows_done, 2)
                    nc.vector.tensor_copy(rows[:, 1, :], ps[:, 1, :]).then_inc(rows_set, 1)
                    dve.wait_ge(turned, 1)
                    by_expert = inv_count[:, 1, :].unsqueeze(1).to_broadcast([P, C, E])
                    nc.vector.tensor_tensor(bn[:, 0, :, :], psT1[0][:, :, :, 0], by_expert, ALU.mult)
                    bn_link(nc.vector.tensor_tensor(bn[:, 1, :, :], psT1[1][:, :, :, 0], by_expert, ALU.mult))
                    bn_link(nc.vector.tensor_tensor(bn[:, 2, :, :], bn[:, 0, :, :], bn[:, 0, :, :], ALU.mult))
                    flat = [bn[:, i, :, :].rearrange("p c e -> p (c e)") for i in range(4)]
                    bn_link(nc.vector.scalar_tensor_tensor(out=flat[1], in0=flat[1], scalar=EPS, in1=flat[2],
                                                           op0=ALU.add, op1=ALU.subtract))
                    low_part(0)
                    dve.wait_ge(bn_root, 1)
                    bn_link(nc.vector.tensor_tensor(bn[:, 2, :, :], bn[:, 1, :, :], gT[:], ALU.mult))
                    bn_link(nc.vector.tensor_tensor(bn[:, 0, :, :], bn[:, 0, :, :], bn[:, 2, :, :], ALU.mult))
                    bn_link(nc.vector.tensor_tensor(bn[:, 3, :, :], bT[:], bn[:, 0, :, :], ALU.subtract))
                    for m in range(1, 4):
                        low_part(m)

                @block.tensor
                def _(pe):
                    def y_products(q):
                        p = q.slot(RING1)
                        pe.wait_ge(x_loaded[p], q.turn(RING1, 16, 16))
                        pe.wait_ge(aT_loaded[p // 2], q.turn(RING1, 32, 32))
                        for t in range(2):
                            if not q.before(2):
                                pe.wait_ge(y_kept[t], q.value(2, -2))
                            for c in range(C):
                                ins = pe.matmul(psY[2 * q.slot(2) + t][:, c, 0:P + 2], x_in[p][:, t, c * P:(c + 1) * P],
                                                aT[:, p, t, :],
                                                start=True, stop=True, skip_group_check=True)
                            ins.then_inc(y_done, 1)

                    pe.wait_ge(aT_ready, 1)
                    steps(pe, y_products, 0, RING1, NQ, NQ - 1, RING1)

                    for t in range(2):
                        pe.wait_ge(y_kept[t], 2 * NQ)
                    pe.wait_ge(small_loaded, 64)
                    for c in range(C):
                        ins = pe.matmul(psSmall[0:B, 0:E], xsum[:, c, :], rw[:, c, :], start=(c == 0), stop=(c == C - 1))
                    ins.then_inc(scored, 1)
                    pe.wait_ge(ids, 7)
                    pe.wait_ge(route, 5)
                    pe.matmul(psRow[:, 0:B], ecol[:, 1:2].to_broadcast([B, P]), ident[0:B, 0:B], start=True, stop=True,
                              skip_group_check=True)
                    pe.matmul(psRow[:, B:B + E], ones[0:B, :].to_broadcast([B, P]), onehot[:], start=True, stop=True,
                              skip_group_check=True).then_inc(route_pe, 1)
                    pe.wait_ge(route, 14)
                    pe.matmul(psSmall[0:1, 0:SLOTS], graph_id[0:B, 0:1], slot_of, start=True, stop=True, skip_group_check=True)
                    pe.matmul(psSmall[0:1, SLOTS:SLOTS + TILES], ecol[:, 1:2], slot_of[:, 0:SLOTS:2], start=True, stop=True,
                              skip_group_check=True)
                    words = SLOTS + TILES
                    pe.matmul(psSmall[0:1, words:words + TILES], graph_id[0:B, 0:1], slot_of[:, 0:SLOTS:2],
                              start=True, stop=False, skip_group_check=True)
                    pe.matmul(psSmall[0:1, words:words + TILES], graph_id[0:B, 1:2], slot_of[:, 1:SLOTS:2],
                              start=False, stop=False, skip_group_check=True)
                    pe.matmul(psSmall[0:1, words + 2:words + TILES], ecol[:, 2:3], slot_of[:, 0:SLOTS - 4:2],
                              start=False, stop=True, skip_group_check=True).then_inc(route_pe, 1)

                    pe.wait_ge(sorted_, 4)
                    pe.wait_ge(w_low, NW)

                    def products(j, t):
                        e = expert_of(pe, j, t)
                        pe.wait_ge(yl_done, j.value(4, 2 * t + 2))
                        if not j.before(1):
                            pe.wait_ge(z_copied, j.value(2, t - 1))
                        n = 0
                        for ya, wa in ((yh, w_h), (yh, w_l), (yl, w_h)):
                            for c in range(C):
                                ins = pe.matmul(psZ[t], ya[:, t, c, :], wa[:, ds(e, 1), c, :].rearrange("p a d -> p (a d)"),
                                                start=(n == 0), stop=(n == 3 * C - 1))
                                n += 1
                        ins.then_inc(z_done, 1)

                    def step(j):
                        products(j, 0)
                        products(j, 1)

                    steps(pe, step, 0, 1, NJ, NJ - 1, 4)

                    pe.wait_ge(z_copied, TILES)
                    for k, sums in enumerate((z_sums, square_sums)):
                        if k == 0:
                            pe.wait_ge(z_summed, TILES)
                        else:
                            pe.wait_ge(sums_set, 2)
                        for e in range(E):
                            part_e = slice(e * (P // E), (e + 1) * (P // E))
                            ins = pe.matmul(ps[part_e, k, :], ones[:].to_broadcast([P, P // E]), sums[:, e, :],
                                            start=True, stop=True, skip_group_check=True)
                        ins.then_inc(rows_done, 1)
                    pe.wait_ge(rows_set, 2)
                    for c in range(C):
                        for k in range(2):
                            ins = pe.transpose(psT1[k][:, c, :, :].rearrange("p e r -> p (e r)"), rows[:, k, c * P:(c + 1) * P],
                                               ident[:])
                    ins.then_inc(turned, 1)
                    for k in range(2):
                        pe.wait_ge(bn_step, 4 if k == 0 else 6)
                        for e in range(E):
                            n = k * E + e
                            if n >= 6:
                                pe.wait_ge(tab_set, n - 5)
                            for c in range(C):
                                ins = pe.matmul(psTab[n % 6][:, c * P:(c + 1) * P], bn[:, 2 + k, c, e:e + 1].to_broadcast([P, P]),
                                                ident[:], start=True, stop=True, skip_group_check=True)
                            ins.then_inc(spread, 1)

        with ExitStack() as st:
            x1 = part(4, 2, D)
            qT = [part(C, 2 * P) for p in range(2)]
            sc = part(2, H, N)
            pT = part(H // 2, P)
            o = part(2, D)
            res = part(2, D)
            adj_in = part(2, N)
            adj2 = part(2, N)
            mx = part(2, H)
            amx = part(2, H)
            tot = part(2, H)
            inv = part(2, H)
            waiter = part(2)
            st1, st2 = part(2, 6), part(2, 6)
            ag1, ag2 = part(2, 2), part(2, 2)
            ve1, ve2 = part(2), part(2)
            rs1, rs2 = part(2), part(2)
            xTh = sb(st, "xTh", [P, C, 2 * P], F32R)
            xTl = sb(st, "xTl", [P, C, 2 * P], F32R)
            oTh = sb(st, "oTh", [P, 2, C, P], F32R)
            oTl = sb(st, "oTl", [P, 2, C, P], F32R)

            RING_XT, RING_Q, RING_K, RING_V, RING_OT, RING_O = (1, 2), (3, 4, 5, 6), (7, 8, 9, 10), (11, 13), (12, 15), (14, 0)

            def ring(use):
                return ps[:, use % 4, :]

            psS = ps[:, 4:6, :].rearrange("p b n -> p (b n)")
            psT = ps[:, 6:8, :].rearrange("p b (k n) -> p (b k) n", n=P)
            psO = ps[:, 4:6, :].rearrange("p b (k g n) -> p (b k) g n", g=2, n=2 * HD)

            zeros2 = sem("zeros2")
            adj_loaded = sem("adj_loaded")
            out_stored = [sem(f"out_stored{t}") for t in range(2)]
            xT_done = sem("xT_done")
            q_done = sem("q_done")
            k_done = sem("k_done")
            v_done = sem("v_done")
            s_done = sem("s_done")
            pT_done = sem("pT_done")
            pv_done = sem("pv_done")
            oT_done = sem("oT_done")
            o_done = sem("o_done")
            xTh_done = sem("xTh_done")
            q_set = sem("q_set")
            k_set = sem("k_set")
            v_set = sem("v_set")
            exp_done = sem("exp_done")
            pT_set = sem("pT_set")
            oTh_done = sem("oTh_done")
            bn_applied = sem("bn_applied")
            bn_first = [sem(f"bn_first{t}") for t in range(2)]
            root1 = sem("root1")
            root2 = sem("root2")
            shifted = sem("shifted")
            relu_res = sem("relu_res")
            stats1 = sem("stats1")
            aggr1 = sem("aggr1")
            var1 = sem("var1")
            x1_done = sem("x1_done")
            xTl_done = sem("xTl_done")
            adj2_done = sem("adj2_done")
            biased = sem("biased")
            max_done = sem("max_done")
            absmax_done = sem("absmax_done")
            tot_done = sem("tot_done")
            tot_inv = sem("tot_inv")
            inv_done = sem("inv_done")
            o_normed = sem("o_normed")
            oTl_done = sem("oTl_done")
            res_done = sem("res_done")
            stats2 = sem("stats2")
            aggr2 = sem("aggr2")
            var2 = sem("var2")
            out_done = sem("out_done")

            def experts(eng, q, t):
                return [eng.value_load(expert[0:1, ds(q.value(4, 2 * t + g), 1)], min_val=0, max_val=E - 1) for g in range(2)]

            def first_batch_norm(eng, ops, t, e):
                for g in range(2):
                    for k, op in enumerate((ALU.mult, ALU.add)):
                        if g or k:
                            eng.wait_ge(bn_first[t], 2 * g + k)
                        rows = slice(g * N, (g + 1) * N)
                        zt = zx[rows, 0, t, :]
                        ins = ops.tensor_tensor(zt, zt, tab[rows, k, ds(e[g], 1), :].rearrange("p a d -> p (a d)"), op)
                        if not (g and k):
                            ins.then_inc(bn_first[t], 1)
                ins.then_inc(bn_applied, 4)

            def pipeline(eng, body, loop_to=NQ - 1):
                def step(s):
                    body(*(s + n if s.i is not None or 0 <= s.k + n < NQ else None for n in (1, 0, -1, -2)))
                steps(eng, step, -1, 3, loop_to, NQ + 1, 4)

            with nc.Block() as block:

                @block.sync
                def _(sp):
                    def store(q, t):
                        sp.wait_ge(out_done, q.value(2, t + 1))
                        sp.dma_start(out_q[ds(q.value(1), 1), t].rearrange("a p d -> (a p) d"), res[:, t, :]
                                     ).then_inc(out_stored[t], 16)

                    def body(a, b, c, d):
                        if b is not None:
                            if not b.before(1):
                                sp.wait_ge(adj2_done, b.value(1))
                            sp.dma_start(adj_in, adj_q[ds(b.value(1), 1)].rearrange("a p t m -> (a p) t m")
                                         ).then_inc(adj_loaded, 16)
                        if d is not None:
                            store(d, 1)
                        if a is not None and (a.i is not None or a.k + 1 < NQ):
                            sp.wait_ge(relu_res, a.value(2, 2))
                            load_zx(sp, a + 1)
                        if c is not None:
                            store(c, 0)

                    pipeline(sp, body, NQ - 5)
                    for t in range(2):
                        sp.wait_ge(out_stored[t], 16 * NQ)

                @block.gpsimd
                def _(pool):
                    def shift(q, t):
                        if q.i is not None or q.k + 2 < NQ:
                            pool.wait_ge(bn_applied, (q + 2).value(8, 4 * t + 4))
                        pool.wait_ge(max_done, q.value(2, t + 1))
                        pool.wait_ge(absmax_done, q.value(2, t + 1))
                        nc.gpsimd.tensor_tensor(sc[:, t, :, :], sc[:, t, :, :],
                                                mx[:, t, :].unsqueeze(2).to_broadcast([P, H, N]),
                                                ALU.subtract).then_inc(shifted, 1)

                    def batch_norm(q, t):
                        e = experts(pool, q, t)
                        pool.wait_ge(zx_loaded, q.value(32, 32))
                        if q.before(1):
                            first_batch_norm(pool, nc.gpsimd, 0, e)
                            return
                        if t == 1 and not q.before(2):
                            pool.wait_ge(shifted, (q + -2).value(2, 1))
                        for k, op in enumerate((ALU.mult, ALU.add)):
                            for g in range(2):
                                rows = slice(g * N, (g + 1) * N)
                                zt = zx[rows, 0, t, :]
                                if k or g:
                                    pool.wait_ge(bn_applied, q.value(8, 4 * t + 2 * k + g))
                                nc.gpsimd.tensor_tensor(zt, zt, tab[rows, k, ds(e[g], 1), :].rearrange("p a d -> p (a d)"),
                                                        op).then_inc(bn_applied, 1)

                    def root(q, t):
                        pool.wait_ge(var2, q.value(2, t + 1))
                        nc.gpsimd.tensor_tensor(rs2[:, t:t + 1], ve2[:, t:t + 1], minus_half[:, 0:1], ALU.pow).then_inc(root2, 1)

                    def body(a, b, c, d):
                        if a is not None:
                            if not a.before(3):
                                pool.wait_ge(root2, (a + -3).value(2, 1))
                            if not a.before(1):
                                pool.wait_ge(root1, a.value(1))
                            batch_norm(a, 0)
                        if c is not None:
                            shift(c, 0)
                        if a is not None and not a.before(1):
                            batch_norm(a, 1)
                        if d is not None:
                            if a is not None:
                                pool.wait_ge(bn_applied, a.value(8, 8))
                            root(d, 1)
                        if c is not None:
                            shift(c, 1)
                        if a is not None:
                            pool.wait_ge(var1, a.value(1, 1))
                            nc.gpsimd.tensor_tensor(rs1, ve1, minus_half[:, 0:2], ALU.pow).then_inc(root1, 1)
                        if c is not None:
                            root(c, 0)

                    pipeline(pool, body)

                @block.scalar
                def _(act):
                    def transposed(b, t):
                        act.wait_ge(xT_done, b.value(2, t + 1))
                        if not b.before(1):
                            act.wait_ge(v_done, b.value(2))
                        nc.scalar.activation(xTh[:, :, t * P:(t + 1) * P], ring(RING_XT[t]).rearrange("p (c n) -> p c n", c=C),
                                             ACT.Copy).then_inc(xTh_done, 1)

                    def q_out(b, c_):
                        act.wait_ge(q_done, b.value(C, c_ + 1))
                        if not b.before(2):
                            act.wait_ge(s_done, b.value(2, -2))
                        nc.scalar.activation(qT[b.slot(2)][:, c_, :], ring(RING_Q[c_])[:, 0:2 * P], ACT.Copy).then_inc(q_set, 1)

                    def k_out(b, c_):
                        act.wait_ge(k_done, b.value(C, c_ + 1))
                        for j in range(HC):
                            rows = slice(j * HD, (j + 1) * HD)
                            ins = nc.scalar.activation(kz[b.slot(2)][rows, c_, :, j * N:(j + 1) * N],
                                                       ring(RING_K[c_])[rows, 0:2 * P].rearrange("p (g n) -> p g n", g=4), ACT.Copy)
                        ins.then_inc(k_set, 1)

                    def v_out(b, t):
                        act.wait_ge(v_done, b.value(2, t + 1))
                        if not b.before(2):
                            act.wait_ge(pv_done, b.value(2, t - 3))
                        for g in range(2):
                            for j in range(2):
                                src = ring(RING_V[t])[g * N:(g + 1) * N, :].rearrange("p (k j d) -> p k j d", j=2, d=HD)[:, :, j, :]
                                ins = nc.scalar.activation(
                                    vz[b.slot(2)][j * N:(j + 1) * N, t, :, g, j * HD:(j + 1) * HD], src, ACT.Copy)
                        ins.then_inc(v_set, 1)

                    def exponential(c, t):
                        act.wait_ge(shifted, c.value(2, t + 1))
                        nc.scalar.activation(sc[:, t, :, :], sc[:, t, :, :], ACT.Exp).then_inc(exp_done, 1)

                    def probs_out(c, t):
                        act.wait_ge(pT_done, c.value(2, t + 1))
                        if not (c.before(1) and t == 0):
                            act.wait_ge(pv_done, c.value(2, t))
                        nc.scalar.activation(pT, psT, ACT.Copy).then_inc(pT_set, 1)

                    def o_transposed(c, t):
                        act.wait_ge(oT_done, c.value(2, t + 1))
                        if not c.before(1):
                            act.wait_ge(o_done, c.value(2, t - 1))
                        nc.scalar.activation(oTh[:, t, :, :], ring(RING_OT[t]).rearrange("p (c n) -> p c n", c=C),
                                             ACT.Copy).then_inc(oTh_done, 1)

                    def body(a, b, c, d):
                        if b is not None:
                            transposed(b, 0)
                            transposed(b, 1)
                        if c is not None:
                            exponential(c, 0)
                        if b is not None:
                            for c_ in range(C):
                                q_out(b, c_)
                            k_out(b, 0)
                            k_out(b, 1)
                        if c is not None:
                            probs_out(c, 0)
                            exponential(c, 1)
                        if b is not None:
                            k_out(b, 2)
                            k_out(b, 3)
                            v_out(b, 0)
                        if c is not None:
                            probs_out(c, 1)
                            o_transposed(c, 0)
                        if b is not None:
                            v_out(b, 1)
                        if c is not None:
                            o_transposed(c, 1)

                    pipeline(act, body)

                @block.vector
                def _(dve):
                    nc.vector.memset(waiter, 0.0).then_inc(zeros2, 1)
                    dve.wait_ge(zeros2, 1)

                    def first_layer(a):
                        slot = a.slot(4)
                        for t in range(2):
                            dve.wait_ge(bn_applied, a.value(8, 8 if a.before(1) else 4 * t + 4))
                            if not a.before(4):
                                dve.wait_ge(res_done, a.value(2, t - 7))
                            nc.vector.scalar_tensor_tensor(out=x1[:, slot, t, :], in0=zx[:, 0, t, :], scalar=0.0,
                                                           in1=zx[:, 1, t, :], op0=ALU.max, op1=ALU.add).then_inc(relu_res, 1)
                            dve.wait_ge(relu_res, a.value(2, t + 1))
                            nc.vector.bn_stats(st1[:, t, :], x1[:, slot, t, :]).then_inc(stats1, 1)
                            dve.wait_ge(stats1, a.value(2, t + 1))
                            nc.vector.tensor_copy(waiter[:, 0:1], waiter[:, 1:2])
                            nc.vector.bn_aggr(ag1[:, t, :], st1[:, t, :]).then_inc(aggr1, 1)
                        dve.wait_ge(aggr1, a.value(2, 2))
                        nc.vector.tensor_scalar(ve1, ag1[:, :, 1], EPS, None, ALU.add).then_inc(var1, 1)

                    def first_norm(a):
                        dve.wait_ge(root1, a.value(1, 1))
                        for t in range(2):
                            xt = x1[:, a.slot(4), t, :]
                            nc.vector.tensor_scalar(xt, xt, ag1[:, t, 0:1], rs1[:, t:t + 1], ALU.subtract, ALU.mult
                                                    ).then_inc(x1_done, 1)

                    def transposed_low(b, t):
                        dve.wait_ge(xTh_done, b.value(2, t + 1))
                        cols = slice(t * P, (t + 1) * P)
                        nc.vector.tensor_tensor(xTl[:, :, cols], ring(RING_XT[t]).rearrange("p (c n) -> p c n", c=C),
                                                xTh[:, :, cols], ALU.subtract).then_inc(xTl_done, 1)

                    def double_adj(c):
                        dve.wait_ge(adj_loaded, c.value(16, 16))
                        if not c.before(1):
                            dve.wait_ge(biased, c.value(2))
                        nc.vector.tensor_tensor(adj2, adj_in, adj_in, ALU.add).then_inc(adj2_done, 1)

                    def add_bias(c, t):
                        dve.wait_ge(s_done, c.value(2, t + 1))
                        if t == 0:
                            dve.wait_ge(adj2_done, c.value(1, 1))
                        if not c.before(1):
                            dve.wait_ge(pT_done, c.value(2, t - 1))
                            dve.wait_ge(tot_done, c.value(2, t - 1))
                        nc.vector.scalar_tensor_tensor(out=sc[:, t, :, :], in0=psS.rearrange("p (h m) -> p h m", m=N), scalar=SCALE,
                                                       in1=adj2[:, t, :].unsqueeze(1).to_broadcast([P, H, N]),
                                                       op0=ALU.mult, op1=ALU.add).then_inc(biased, 1)

                    def maxima(c, t):
                        dve.wait_ge(biased, c.value(2, t + 1))
                        if not c.before(1):
                            dve.wait_ge(shifted, c.value(2, t - 1))
                            dve.wait_ge(inv_done, c.value(2, t - 1))
                        nc.vector.tensor_reduce(mx[:, t, :], sc[:, t, :, :], AX.X, ALU.max).then_inc(max_done, 1)
                        nc.vector.tensor_reduce(amx[:, t, :], sc[:, t, :, :], AX.X, ALU.max,
                                                apply_absolute_value=True).then_inc(absmax_done, 1)

                    def totals(c, t):
                        dve.wait_ge(exp_done, c.value(2, t + 1))
                        if not c.before(1):
                            dve.wait_ge(inv_done, c.value(2, t - 1))
                        nc.vector.tensor_reduce(tot[:, t, :], sc[:, t, :, :], AX.X, ALU.add).then_inc(tot_done, 1)
                        dve.wait_ge(tot_done, c.value(2, t + 1))
                        if not c.before(1):
                            dve.wait_ge(o_normed, c.value(4, 2 * t - 2))
                        nc.vector.reciprocal(inv[:, t, :], tot[:, t, :]).then_inc(tot_inv, 1)
                        dve.wait_ge(tot_inv, c.value(2, t + 1))
                        nc.vector.scalar_tensor_tensor(out=inv[:, t, :], in0=amx[:, t, :], scalar=0.0, in1=inv[:, t, :],
                                                       op0=ALU.is_gt, op1=ALU.mult).then_inc(inv_done, 1)

                    def normalise(c, t):
                        dve.wait_ge(pv_done, c.value(2, t + 1))
                        dve.wait_ge(inv_done, c.value(2, t + 1))
                        if not c.before(1):
                            dve.wait_ge(oT_done, c.value(2, t - 1))
                        for g in range(2):
                            rows = slice(g * N, (g + 1) * N)
                            nc.vector.tensor_tensor(
                                o[rows, t, :].rearrange("p (k j d) -> p k j d", j=2, d=HD),
                                psO[rows, :, g, :].rearrange("p k (j d) -> p k j d", d=HD),
                                inv[rows, t, :].rearrange("p (k j) -> p k j", j=2).unsqueeze(3).to_broadcast([N, H // 2, 2, HD]),
                                ALU.mult).then_inc(o_normed, 1)

                    def o_transposed_low(c, t):
                        dve.wait_ge(oTh_done, c.value(2, t + 1))
                        nc.vector.tensor_tensor(oTl[:, t, :, :], ring(RING_OT[t]).rearrange("p (c n) -> p c n", c=C),
                                                oTh[:, t, :, :], ALU.subtract).then_inc(oTl_done, 1)

                    def second_residual(c, t):
                        dve.wait_ge(o_done, c.value(2, t + 1))
                        if not c.before(1):
                            dve.wait_ge(out_stored[t], c.value(16))
                        nc.vector.tensor_tensor(res[:, t, :], ring(RING_O[t]), x1[:, c.slot(4), t, :], ALU.add).then_inc(res_done, 1)
                        dve.wait_ge(res_done, c.value(2, t + 1))
                        nc.vector.bn_stats(st2[:, t, :], res[:, t, :]).then_inc(stats2, 1)
                        dve.wait_ge(stats2, c.value(2, t + 1))
                        nc.vector.tensor_copy(waiter[:, 0:1], waiter[:, 1:2])
                        nc.vector.bn_aggr(ag2[:, t, :], st2[:, t, :]).then_inc(aggr2, 1)
                        dve.wait_ge(aggr2, c.value(2, t + 1))
                        nc.vector.tensor_scalar(ve2[:, t:t + 1], ag2[:, t, 1:2], EPS, None, ALU.add).then_inc(var2, 1)

                    def second_norm(c, t):
                        dve.wait_ge(root2, c.value(2, t + 1))
                        nc.vector.tensor_scalar(res[:, t, :], res[:, t, :], ag2[:, t, 0:1], rs2[:, t:t + 1],
                                                ALU.subtract, ALU.mult).then_inc(out_done, 1)

                    e = experts(dve, Number(0), 1)
                    dve.wait_ge(zx_loaded, 32)
                    first_batch_norm(dve, nc.vector, 1, e)

                    def body(a, b, c, d):
                        if c is not None:
                            double_adj(c)
                            add_bias(c, 0)
                        if b is not None:
                            transposed_low(b, 0)
                            transposed_low(b, 1)
                        if c is not None:
                            maxima(c, 0)
                        if d is not None:
                            second_residual(d, 1)
                        if c is not None:
                            add_bias(c, 1)
                            maxima(c, 1)
                            totals(c, 0)
                        if d is not None:
                            second_norm(d, 1)
                        if a is not None:
                            first_layer(a)
                        if c is not None:
                            normalise(c, 0)
                            totals(c, 1)
                        if a is not None:
                            first_norm(a)
                        if c is not None:
                            o_transposed_low(c, 0)
                            normalise(c, 1)
                            second_residual(c, 0)
                            o_transposed_low(c, 1)
                            second_norm(c, 0)

                    pipeline(dve, body)

                @block.tensor
                def _(pe):
                    def split_product(dst, lhs_h, lhs_l, rhs_h, rhs_l):
                        n = 0
                        for lhs, rhs in ((lhs_h, rhs_h), (lhs_h, rhs_l), (lhs_l, rhs_h)):
                            for c_ in range(C):
                                ins = pe.matmul(dst, lhs(c_), rhs(c_), start=(n == 0), stop=(n == 3 * C - 1))
                                n += 1
                        return ins

                    def transposes(b, t):
                        pe.wait_ge(x1_done, b.value(2, t + 1))
                        if t == 0 and not b.before(1):
                            pe.wait_ge(v_set, b.value(2))
                        elif t == 1 and not b.before(2):
                            pe.wait_ge(res_done, b.value(2, -3))
                        elif t == 1 and not b.before(1):
                            pe.wait_ge(k_set, C)
                        for c_ in range(C):
                            ins = pe.transpose(ring(RING_XT[t])[:, c_ * P:(c_ + 1) * P],
                                               x1[:, b.slot(4), t, c_ * P:(c_ + 1) * P], ident[:])
                        ins.then_inc(xT_done, 1)

                    def scores(c, t):
                        if t == 0:
                            pe.wait_ge(q_set, c.value(C, C))
                            pe.wait_ge(k_set, c.value(C, C))
                            if not c.before(1):
                                pe.wait_ge(o_normed, c.value(4))
                        else:
                            pe.wait_ge(biased, c.value(2, 1))
                        p = c.slot(2)
                        for c_ in range(C):
                            for g in range(2):
                                rows = slice(g * N, (g + 1) * N)
                                ins = pe.matmul(psS[rows, c_ * HC * N:(c_ + 1) * HC * N],
                                                qT[p][:, c_, t * P + g * N:t * P + (g + 1) * N], kz[p][:, c_, 2 * t + g, :],
                                                start=True, stop=True, skip_group_check=True)
                        ins.then_inc(s_done, 1)

                    def project(b, w, c_, uses, done, free, value):
                        pe.wait_ge(free, value)
                        cols = slice(c_ * P, (c_ + 1) * P)
                        split_product(ring(uses[c_])[:, 0:2 * P], lambda i: w_h[:, w, i, cols], lambda i: w_l[:, w, i, cols],
                                      lambda i: xTh[:, i, :], lambda i: xTl[:, i, :]).then_inc(done, 1)

                    def values(b, t):
                        pe.wait_ge(k_set, b.value(C, 1 if t == 0 else 3))
                        cols = slice(t * P, (t + 1) * P)
                        split_product(ring(RING_V[t]), lambda i: xTh[:, i, cols], lambda i: xTl[:, i, cols],
                                      lambda i: w_h[:, 2, i, :], lambda i: w_l[:, 2, i, :]).then_inc(v_done, 1)

                    def prob_transposes(c, t):
                        pe.wait_ge(exp_done, c.value(2, t + 1))
                        if not (c.before(1) and t == 0):
                            pe.wait_ge(pT_set, c.value(2, t))
                        for k in range(H // 2):
                            ins = pe.transpose(psT[:, k, :], sc[:, t, 2 * k:2 * k + 2, :].rearrange("p h m -> p (h m)"), ident[:])
                        ins.then_inc(pT_done, 1)

                    def attend(c, t):
                        pe.wait_ge(pT_set, c.value(2, t + 1))
                        pe.wait_ge(v_set, c.value(2, t + 1))
                        if t == 0:
                            pe.wait_ge(biased, c.value(2, 2))
                        else:
                            pe.wait_ge(o_normed, c.value(4, 2))
                        for k in range(H // 2):
                            ins = pe.matmul(psO[:, k, :, :].rearrange("p g n -> p (g n)"), pT[:, k, :],
                                            vz[c.slot(2)][:, t, k, :, :].rearrange("p g n -> p (g n)"), start=True, stop=True)
                        ins.then_inc(pv_done, 1)

                    def o_transposes(c, t, last):
                        pe.wait_ge(o_normed, c.value(4, 2 * t + 2))
                        pe.wait_ge(*last)
                        for c_ in range(C):
                            ins = pe.transpose(ring(RING_OT[t])[:, c_ * P:(c_ + 1) * P], o[:, t, c_ * P:(c_ + 1) * P], ident[:])
                        ins.then_inc(oT_done, 1)

                    def output(c, t, last):
                        pe.wait_ge(oTl_done, c.value(2, t + 1))
                        pe.wait_ge(*last)
                        split_product(ring(RING_O[t]), lambda i: oTh[:, t, i, :], lambda i: oTl[:, t, i, :],
                                      lambda i: w_h[:, 3, i, :], lambda i: w_l[:, 3, i, :]).then_inc(o_done, 1)

                    def body(a, b, c, d):
                        if c is not None:
                            scores(c, 0)
                        if b is not None:
                            transposes(b, 0)
                            transposes(b, 1)
                        if d is not None:
                            output(d, 1, (oTl_done, d.value(2, 1)))
                        if c is not None:
                            scores(c, 1)
                        if b is not None:
                            pe.wait_ge(xTl_done, b.value(2, 2))
                            if not b.before(2):
                                free = ((oTl_done, b.value(2, -2)), (res_done, b.value(2, -2)))
                            elif not b.before(1):
                                free = ((v_set, 1), (k_set, 2))
                            else:
                                free = ((xTl_done, 1), (xTl_done, 1))
                            free += ((xTl_done, b.value(2, 1)), (xTl_done, b.value(2, 2)))
                            for c_ in range(C):
                                project(b, 0, c_, RING_Q, q_done, *free[c_])
                            for c_ in range(2):
                                project(b, 1, c_, RING_K, k_done, q_set, b.value(C, c_ + 1))
                        if c is not None:
                            prob_transposes(c, 0)
                        if b is not None:
                            for c_ in range(2, C):
                                project(b, 1, c_, RING_K, k_done, q_set, b.value(C, c_ + 1))
                        if c is not None:
                            attend(c, 0)
                        if b is not None:
                            values(b, 0)
                        if c is not None:
                            prob_transposes(c, 1)
                            o_transposes(c, 0, (k_set, b.value(C, 2)) if b is not None else (res_done, c.value(2)))
                        if b is not None:
                            values(b, 1)
                        if c is not None:
                            attend(c, 1)
                            output(c, 0, (k_set, b.value(C, 4)) if b is not None else (res_done, c.value(2, -1)))
                            o_transposes(c, 1, (v_set, b.value(2, 1)) if b is not None else (oTl_done, c.value(2)))

                    pipeline(pe, body)


_IN = ["x", "adj", "adjT", "router_w", "router_b", "expert_w", "gammaT", "betaT", "wqT", "wkT", "wvT", "woT"]


def kernel(x, adj, L0_gnn_router_w, L0_gnn_router_b, L0_gnn_expert_w, L0_gnn_bn_gamma, L0_gnn_bn_beta,
           L1_gnn_Wq, L1_gnn_Wk, L1_gnn_Wv, L1_gnn_Wo):
    import concourse.bacc as bacc
    from concourse.bass_utils import run_bass_kernel_spmd

    laid_out = dict(
        x=x, adj=adj, adjT=np.swapaxes(adj, 1, 2), router_w=L0_gnn_router_w, router_b=L0_gnn_router_b,
        expert_w=L0_gnn_expert_w, gammaT=np.swapaxes(L0_gnn_bn_gamma, 0, 1), betaT=np.swapaxes(L0_gnn_bn_beta, 0, 1),
        wqT=np.swapaxes(L1_gnn_Wq, 0, 1), wkT=np.swapaxes(L1_gnn_Wk, 0, 1),
        wvT=np.swapaxes(L1_gnn_Wv, 0, 1), woT=np.swapaxes(L1_gnn_Wo, 0, 1),
    )
    nc = bacc.Bacc("TRN2", target_bir_lowering=False, num_devices=1, dynamic_dma_scratch_size=1024)
    arrays, args = {}, []
    for name in _IN:
        a = np.ascontiguousarray(laid_out[name])
        arrays[f"in_{name}"] = a
        args.append(nc.dram_tensor(f"in_{name}", a.shape, mybir.dt.from_np(a.dtype), kind="ExternalInput").ap())
    args.append(nc.dram_tensor("out_0", x.shape, F32, kind="ExternalOutput").ap())
    graph_layers(nc, *args)
    r = run_bass_kernel_spmd(nc, [arrays], core_ids=[0])
    return r.results[0]["out_0"]
```
